# Optimizing a Trainium2 kernel written in Bass

```python
import numpy as np
import jax
import jax.numpy as jnp

def _softmax(x, axis=-1):
    return jax.nn.softmax(x, axis=axis)

def _gelu(x):
    return jax.nn.gelu(x, approximate=True)

def _silu(x):
    return jax.nn.silu(x)

def _sigmoid(x):
    return jax.nn.sigmoid(x)

def _layernorm(x, axis=-1, eps=1e-05):
    m = jnp.mean(x, axis=axis, keepdims=True)
    v = jnp.var(x, axis=axis, keepdims=True)
    return (x - m) / jnp.sqrt(v + eps)

def _scatter_add(tgt, idx, src, axis=0):
    return tgt.at[idx].add(src)

def _segment_sum(src, seg, n):
    return jax.ops.segment_sum(src, seg, n)
kernel_name = 'mk_dlrm_tower_d1_rec_r8_5099cc'

def setup_inputs(seed: int=0):
    np.random.seed(seed)
    _w = jnp.asarray

    def _rec_inputs():
        import jax
        import jax.numpy as jnp
        _tk = jax.random.key(seed)
        dense_ctx = jax.random.normal(jax.random.fold_in(_tk, 190), (1024, 16), jnp.float32)
        ids = jnp.stack([jax.random.randint(jax.random.fold_in(_tk, 200 + f), (1024,), 0, v, jnp.int32) for f, v in enumerate([125000, 125000, 125000, 1250, 1000, 1000, 12500, 12500, 1000, 12500, 1000, 1250, 12500, 1250, 1000, 1250, 1000, 12500, 12500, 12500, 12500, 1250, 1000, 1000, 1250, 1000, 1250, 1000, 1250, 1250, 1000, 1000])], axis=1)
        tbl_0 = 0.05 * jax.random.normal(jax.random.fold_in(_tk, 500 + 0), (125000, 64), jnp.float32)
        tbl_1 = 0.05 * jax.random.normal(jax.random.fold_in(_tk, 500 + 1), (125000, 64), jnp.float32)
        tbl_2 = 0.05 * jax.random.normal(jax.random.fold_in(_tk, 500 + 2), (125000, 64), jnp.float32)
        tbl_3 = 0.05 * jax.random.normal(jax.random.fold_in(_tk, 500 + 3), (1250, 64), jnp.float32)
        tbl_4 = 0.05 * jax.random.normal(jax.random.fold_in(_tk, 500 + 4), (1000, 64), jnp.float32)
        tbl_5 = 0.05 * jax.random.normal(jax.random.fold_in(_tk, 500 + 5), (1000, 64), jnp.float32)
        tbl_6 = 0.05 * jax.random.normal(jax.random.fold_in(_tk, 500 + 6), (12500, 64), jnp.float32)
        tbl_7 = 0.05 * jax.random.normal(jax.random.fold_in(_tk, 500 + 7), (12500, 64), jnp.float32)
        tbl_8 = 0.05 * jax.random.normal(jax.random.fold_in(_tk, 500 + 8), (1000, 64), jnp.float32)
        tbl_9 = 0.05 * jax.random.normal(jax.random.fold_in(_tk, 500 + 9), (12500, 64), jnp.float32)
        tbl_10 = 0.05 * jax.random.normal(jax.random.fold_in(_tk, 500 + 10), (1000, 64), jnp.float32)
        tbl_11 = 0.05 * jax.random.normal(jax.random.fold_in(_tk, 500 + 11), (1250, 64), jnp.float32)
        tbl_12 = 0.05 * jax.random.normal(jax.random.fold_in(_tk, 500 + 12), (12500, 64), jnp.float32)
        tbl_13 = 0.05 * jax.random.normal(jax.random.fold_in(_tk, 500 + 13), (1250, 64), jnp.float32)
        tbl_14 = 0.05 * jax.random.normal(jax.random.fold_in(_tk, 500 + 14), (1000, 64), jnp.float32)
        tbl_15 = 0.05 * jax.random.normal(jax.random.fold_in(_tk, 500 + 15), (1250, 64), jnp.float32)
        tbl_16 = 0.05 * jax.random.normal(jax.random.fold_in(_tk, 500 + 16), (1000, 64), jnp.float32)
        tbl_17 = 0.05 * jax.random.normal(jax.random.fold_in(_tk, 500 + 17), (12500, 64), jnp.float32)
        tbl_18 = 0.05 * jax.random.normal(jax.random.fold_in(_tk, 500 + 18), (12500, 64), jnp.float32)
        tbl_19 = 0.05 * jax.random.normal(jax.random.fold_in(_tk, 500 + 19), (12500, 64), jnp.float32)
        tbl_20 = 0.05 * jax.random.normal(jax.random.fold_in(_tk, 500 + 20), (12500, 64), jnp.float32)
        tbl_21 = 0.05 * jax.random.normal(jax.random.fold_in(_tk, 500 + 21), (1250, 64), jnp.float32)
        tbl_22 = 0.05 * jax.random.normal(jax.random.fold_in(_tk, 500 + 22), (1000, 64), jnp.float32)
        tbl_23 = 0.05 * jax.random.normal(jax.random.fold_in(_tk, 500 + 23), (1000, 64), jnp.float32)
        tbl_24 = 0.05 * jax.random.normal(jax.random.fold_in(_tk, 500 + 24), (1250, 64), jnp.float32)
        tbl_25 = 0.05 * jax.random.normal(jax.random.fold_in(_tk, 500 + 25), (1000, 64), jnp.float32)
        tbl_26 = 0.05 * jax.random.normal(jax.random.fold_in(_tk, 500 + 26), (1250, 64), jnp.float32)
        tbl_27 = 0.05 * jax.random.normal(jax.random.fold_in(_tk, 500 + 27), (1000, 64), jnp.float32)
        tbl_28 = 0.05 * jax.random.normal(jax.random.fold_in(_tk, 500 + 28), (1250, 64), jnp.float32)
        tbl_29 = 0.05 * jax.random.normal(jax.random.fold_in(_tk, 500 + 29), (1250, 64), jnp.float32)
        tbl_30 = 0.05 * jax.random.normal(jax.random.fold_in(_tk, 500 + 30), (1000, 64), jnp.float32)
        tbl_31 = 0.05 * jax.random.normal(jax.random.fold_in(_tk, 500 + 31), (1000, 64), jnp.float32)
        _rk = jax.random.fold_in(_tk, 7)
        W_top1 = 0.0693375 * jax.random.normal(jax.random.fold_in(_tk, 801), (208, 512), jnp.float32)
        W_top2 = 0.0441942 * jax.random.normal(jax.random.fold_in(_tk, 802), (512, 256), jnp.float32)
        W_top3 = 0.0625 * jax.random.normal(jax.random.fold_in(_tk, 803), (256, 1), jnp.float32)
        b_top1 = jnp.zeros((512,), jnp.float32)
        b_top2 = jnp.zeros((256,), jnp.float32)
        return (dense_ctx, ids, tbl_0, tbl_1, tbl_2, tbl_3, tbl_4, tbl_5, tbl_6, tbl_7, tbl_8, tbl_9, tbl_10, tbl_11, tbl_12, tbl_13, tbl_14, tbl_15, tbl_16, tbl_17, tbl_18, tbl_19, tbl_20, tbl_21, tbl_22, tbl_23, tbl_24, tbl_25, tbl_26, tbl_27, tbl_28, tbl_29, tbl_30, tbl_31, W_top1, b_top1, W_top2, b_top2, W_top3)
    dense_ctx, ids, tbl_0, tbl_1, tbl_2, tbl_3, tbl_4, tbl_5, tbl_6, tbl_7, tbl_8, tbl_9, tbl_10, tbl_11, tbl_12, tbl_13, tbl_14, tbl_15, tbl_16, tbl_17, tbl_18, tbl_19, tbl_20, tbl_21, tbl_22, tbl_23, tbl_24, tbl_25, tbl_26, tbl_27, tbl_28, tbl_29, tbl_30, tbl_31, W_top1, b_top1, W_top2, b_top2, W_top3 = _rec_inputs()

    def _L0_rec_setup():
        import jax, jax.numpy as jnp
        import numpy as np
        B, F_SIZE, DIM = (256, 32, 64)
        LAYER_SIZES = (128, 128)

        def _cin_forward(inputs, Ws, bs):
            batch, _, dim = inputs.shape
            x0 = inputs
            h = inputs
            finals = []
            n_layers = len(Ws)
            for i in range(n_layers):
                H = h.shape[1]
                M = x0.shape[1]
                z = jnp.einsum('bhd,bmd->bhmd', h, x0).reshape(batch, H * M, dim)
                out = jnp.einsum('bcd,oc->bod', z, Ws[i]) + bs[i][None, :, None]
                out = jax.nn.relu(out)
                size = Ws[i].shape[0]
                if i != n_layers - 1:
                    h = out[:, :size // 2, :]
                    finals.append(out[:, size // 2:, :])
                else:
                    finals.append(out)
            result = jnp.concatenate(finals, axis=1)
            return jnp.sum(result, axis=-1)
        key = jax.random.key(seed)
        k1, k2, k3 = jax.random.split(key, 3)
        inputs = jax.random.normal(k1, (B, F_SIZE, DIM), dtype=jnp.float32)
        W0 = jax.random.normal(k2, (128, F_SIZE * F_SIZE), dtype=jnp.float32) * 0.03
        b0 = jnp.zeros((128,), dtype=jnp.float32)
        W1 = jax.random.normal(k3, (128, 64 * F_SIZE), dtype=jnp.float32) * 0.03
        b1 = jnp.zeros((128,), dtype=jnp.float32)
        return {'inputs': inputs, 'W0': W0, 'b0': b0, 'W1': W1, 'b1': b1}
    _L0_rec_all = _L0_rec_setup()
    _L0_rec_in = {k: v for k, v in _L0_rec_all.items() if k in ('W0', 'b0', 'W1', 'b1')}
    del _L0_rec_all
    return {'dense_ctx': dense_ctx, 'ids': ids, 'tbl_0': tbl_0, 'tbl_1': tbl_1, 'tbl_2': tbl_2, 'tbl_3': tbl_3, 'tbl_4': tbl_4, 'tbl_5': tbl_5, 'tbl_6': tbl_6, 'tbl_7': tbl_7, 'tbl_8': tbl_8, 'tbl_9': tbl_9, 'tbl_10': tbl_10, 'tbl_11': tbl_11, 'tbl_12': tbl_12, 'tbl_13': tbl_13, 'tbl_14': tbl_14, 'tbl_15': tbl_15, 'tbl_16': tbl_16, 'tbl_17': tbl_17, 'tbl_18': tbl_18, 'tbl_19': tbl_19, 'tbl_20': tbl_20, 'tbl_21': tbl_21, 'tbl_22': tbl_22, 'tbl_23': tbl_23, 'tbl_24': tbl_24, 'tbl_25': tbl_25, 'tbl_26': tbl_26, 'tbl_27': tbl_27, 'tbl_28': tbl_28, 'tbl_29': tbl_29, 'tbl_30': tbl_30, 'tbl_31': tbl_31, 'W_top1': W_top1, 'b_top1': b_top1, 'W_top2': W_top2, 'b_top2': b_top2, 'W_top3': W_top3, 'L0_rec_W0': _L0_rec_in['W0'], 'L0_rec_b0': _L0_rec_in['b0'], 'L0_rec_W1': _L0_rec_in['W1'], 'L0_rec_b1': _L0_rec_in['b1']}

def reference(dense_ctx, ids, tbl_0, tbl_1, tbl_2, tbl_3, tbl_4, tbl_5, tbl_6, tbl_7, tbl_8, tbl_9, tbl_10, tbl_11, tbl_12, tbl_13, tbl_14, tbl_15, tbl_16, tbl_17, tbl_18, tbl_19, tbl_20, tbl_21, tbl_22, tbl_23, tbl_24, tbl_25, tbl_26, tbl_27, tbl_28, tbl_29, tbl_30, tbl_31, W_top1, b_top1, W_top2, b_top2, W_top3, L0_rec_W0, L0_rec_b0, L0_rec_W1, L0_rec_b1):
    import jax
    import jax.numpy as jnp

    def _L0_rec_ref(inputs, W0, b0, W1, b1):
        import jax, jax.numpy as jnp
        import numpy as np
        B, F_SIZE, DIM = (256, 32, 64)
        LAYER_SIZES = (128, 128)

        def _cin_forward(inputs, Ws, bs):
            batch, _, dim = inputs.shape
            x0 = inputs
            h = inputs
            finals = []
            n_layers = len(Ws)
            for i in range(n_layers):
                H = h.shape[1]
                M = x0.shape[1]
                z = jnp.einsum('bhd,bmd->bhmd', h, x0).reshape(batch, H * M, dim)
                out = jnp.einsum('bcd,oc->bod', z, Ws[i]) + bs[i][None, :, None]
                out = jax.nn.relu(out)
                size = Ws[i].shape[0]
                if i != n_layers - 1:
                    h = out[:, :size // 2, :]
                    finals.append(out[:, size // 2:, :])
                else:
                    finals.append(out)
            result = jnp.concatenate(finals, axis=1)
            return jnp.sum(result, axis=-1)
        return _cin_forward(inputs, (W0, W1), (b0, b1))
    e = jnp.stack([tbl_0[ids[:, 0]], tbl_1[ids[:, 1]], tbl_2[ids[:, 2]], tbl_3[ids[:, 3]], tbl_4[ids[:, 4]], tbl_5[ids[:, 5]], tbl_6[ids[:, 6]], tbl_7[ids[:, 7]], tbl_8[ids[:, 8]], tbl_9[ids[:, 9]], tbl_10[ids[:, 10]], tbl_11[ids[:, 11]], tbl_12[ids[:, 12]], tbl_13[ids[:, 13]], tbl_14[ids[:, 14]], tbl_15[ids[:, 15]], tbl_16[ids[:, 16]], tbl_17[ids[:, 17]], tbl_18[ids[:, 18]], tbl_19[ids[:, 19]], tbl_20[ids[:, 20]], tbl_21[ids[:, 21]], tbl_22[ids[:, 22]], tbl_23[ids[:, 23]], tbl_24[ids[:, 24]], tbl_25[ids[:, 25]], tbl_26[ids[:, 26]], tbl_27[ids[:, 27]], tbl_28[ids[:, 28]], tbl_29[ids[:, 29]], tbl_30[ids[:, 30]], tbl_31[ids[:, 31]]], axis=1)
    z = _L0_rec_ref(e, L0_rec_W0, L0_rec_b0, L0_rec_W1, L0_rec_b1)
    z = z.reshape(z.shape[0], -1)
    h = jnp.concatenate([z, dense_ctx], axis=1)
    h = jnp.maximum(h @ W_top1 + b_top1, 0.0)
    h = jnp.maximum(h @ W_top2 + b_top2, 0.0)
    y = h @ W_top3
    return y

_drawn_inputs = setup_inputs


def setup_inputs(seed=0):
    import zlib

    import numpy as np

    out = dict(_drawn_inputs(seed))
    spreads = {'b_top1': (0.0, 2.0),
     'b_top2': (0.0, 2.0),
     'L0_rec_b0': (0.0, 0.1),
     'L0_rec_b1': (0.0, 0.568)}
    factors = {'tbl_0': 8.0,
     'tbl_1': 8.0,
     'tbl_2': 8.0,
     'tbl_3': 8.0,
     'tbl_4': 8.0,
     'tbl_5': 8.0,
     'tbl_6': 8.0,
     'tbl_7': 8.0,
     'tbl_8': 8.0,
     'tbl_9': 8.0,
     'tbl_10': 8.0,
     'tbl_11': 8.0,
     'tbl_12': 8.0,
     'tbl_13': 8.0,
     'tbl_14': 8.0,
     'tbl_15': 8.0,
     'tbl_16': 8.0,
     'tbl_17': 8.0,
     'tbl_18': 8.0,
     'tbl_19': 8.0,
     'tbl_20': 8.0,
     'tbl_21': 8.0,
     'tbl_22': 8.0,
     'tbl_23': 8.0,
     'tbl_24': 8.0,
     'tbl_25': 8.0,
     'tbl_26': 8.0,
     'tbl_27': 8.0,
     'tbl_28': 8.0,
     'tbl_29': 8.0,
     'tbl_30': 8.0,
     'tbl_31': 8.0,
     'L0_rec_W0': 8.0,
     'L0_rec_W1': 7.693,
     'dense_ctx': 8.0}
    for name, (base, spread) in spreads.items():
        noise = np.random.default_rng([zlib.crc32(name.encode()), seed]).standard_normal(out[name].shape)
        drawn = base * np.exp(spread * noise) if base else spread * noise
        out[name] = jnp.asarray(drawn.astype(out[name].dtype))
    for name, factor in factors.items():
        out[name] = (out[name] * factor).astype(out[name].dtype)
    return out
```

```python
import numpy as np
import concourse.bass as bass
from concourse import mybir
from contextlib import ExitStack

F32 = mybir.dt.float32
I32 = mybir.dt.int32
ALU = mybir.AluOpType
ACT = mybir.ActivationFunctionType
AX = mybir.AxisListType

P = 128
BATCH, FIELDS, DIM, DENSE = 1024, 32, 64, 16
OUT = 128
HID = OUT // 2
QUADS = P // FIELDS
ROWS = 16
COLS = ROWS * DIM
BLOCKS = BATCH // ROWS
BANK = 512
HALVES = COLS // BANK
ROTS = FIELDS // QUADS
L0_FULL = ROTS // 2
LEFT = FIELDS // 2
L0_STEPS = L0_FULL + 1
HBLKS = HID // FIELDS
L1_STEPS = ROTS * HBLKS
STEPS = L0_STEPS + L1_STEPS
RING = 6
TILES = BATCH // P
TILE_BLOCKS = P // ROWS
PITCH = BATCH * DIM + 1024
H1, H2 = 512, 256
C1, C2 = H1 // P, H2 // P
MN = BATCH // BANK



def l0_base(n):
    return L0_STEPS + (n - 1) * STEPS


def l1_base(n):
    return n * STEPS + 2 * L0_STEPS


def cin_mlp(nc, ids, dense_t, w0_first, w0_second, w0_left, w1, b0, b1, w_top1, b_top1, w_top2, b_top2, w_top3,
            tables, y):
    ctx = ExitStack()
    with ctx:
        def sb(name, shape, dt=F32):
            return ctx.enter_context(nc.sbuf_tensor(name, shape, dt))

        def pb(name, shape):
            return ctx.enter_context(nc.psum_tensor(name, shape, F32))

        def sem(name):
            return ctx.enter_context(nc.semaphore(name))

        fields_dram = nc.dram_tensor("fields_dram", (2 * FIELDS, PITCH), F32).ap()

        idx = [sb(f"idx{b}", [P, FIELDS], I32) for b in range(2)]
        emb = [sb(f"emb{b}", [P, FIELDS * DIM]) for b in range(2)]
        rot = [[sb(f"rot{b}_{k}", [P, COLS]) for k in range(ROTS)] for b in range(2)]
        xrep = [sb(f"xrep{b}", [P, COLS]) for b in range(2)]
        hrep = [[sb(f"hrep{b}_{j}", [P, COLS]) for j in range(HBLKS)] for b in range(2)]
        prod = [sb(f"prod{r}", [P, COLS]) for r in range(RING)]
        relu0 = sb("relu0", [P, COLS])
        relu1 = sb("relu1", [P, COLS])
        w0_sb = sb("w0_sb", [P, L0_FULL, OUT])
        w0b_sb = sb("w0b_sb", [P, L0_FULL, OUT])
        w0l_sb = sb("w0l_sb", [LEFT, 2, OUT])
        w1_sb = sb("w1_sb", [P, L1_STEPS, OUT])
        b0_sb = sb("b0_sb", [P, 1])
        b1_sb = sb("b1_sb", [P, 1])
        wt1_sb = sb("wt1_sb", [P, 2, H1])
        bt1_sb = sb("bt1_sb", [P, C1])
        wt2_sb = sb("wt2_sb", [P, C1, H2])
        bt2_sb = sb("bt2_sb", [P, C2])
        wt3_sb = sb("wt3_sb", [P, C2])
        feat0 = sb("feat0", [P, BATCH])
        feat1 = sb("feat1", [P, BATCH])
        h2_sb = sb("h2_sb", [P, C2, BATCH])
        y_sb = sb("y_sb", [1, BATCH])
        h1_sb = prod

        out0 = pb("out0", [P, COLS])
        out1 = pb("out1", [P, COLS])
        mlp_ps = pb("mlp_ps", [P, 2 * COLS])
        banks = [mlp_ps[:, j * BANK:(j + 1) * BANK] for j in range(4)] + \
                [out0[:, j * BANK:(j + 1) * BANK] for j in range(2)] + \
                [out1[:, j * BANK:(j + 1) * BANK] for j in range(2)]

        idx_loaded = [sem(f"idx_loaded{b}") for b in range(2)]
        gathered = [sem(f"gathered{b}") for b in range(2)]
        tile_started = sem("tile_started")
        scratch_written = sem("scratch_written")
        xrep_loaded = [sem(f"xrep_loaded{b}") for b in range(2)]
        rot_loaded = [[sem(f"rot_loaded{b}_{k}") for k in range(ROTS)] for b in range(2)]
        w0_loaded = sem("w0_loaded")
        w1_loaded = sem("w1_loaded")
        bias_loaded = sem("bias_loaded")
        top_loaded = sem("top_loaded")
        w0_folded = sem("w0_folded")
        zeroed = sem("zeroed")
        prod_made = sem("prod_made")
        prod_used = sem("prod_used")
        relu0_made = sem("relu0_made")
        relu1_made = sem("relu1_made")
        hrep_made = sem("hrep_made")
        sum0_made = sem("sum0_made")
        sum1_made = sem("sum1_made")
        h1_done = sem("h1_done")
        h1_made = sem("h1_made")
        h2_done = sem("h2_done")
        h2_made = sem("h2_made")
        y_done = sem("y_done")
        y_made = sem("y_made")
        y_stored = sem("y_stored")

        block = ctx.enter_context(nc.Block())

        @block.gpsimd
        def _(pool):
            def gather(t, b, nth):
                pool.dma_start(idx[b][:, :], ids[bass.ds(t * P, P), :]).then_inc(idx_loaded[b], 16)
                pool.wait_ge(idx_loaded[b], nth * 16)
                pool.sem_inc(tile_started, 1)
                for f in range(FIELDS):
                    pool.indirect_dma_start(
                        out=emb[b][:, f * DIM:(f + 1) * DIM], out_offset=None, in_=tables[f],
                        in_offset=bass.IndirectOffsetOnAxis(ap=idx[b][:, f:f + 1], axis=0),
                    ).then_inc(gathered[b], 16)

            pool.memset(feat0[:, :], 0.0).then_inc(zeroed, 1)
            for t in range(2):
                gather(t, t, 1)
            with pool.Fori(1, TILES // 2) as pair:
                for b in range(2):
                    pool.wait_ge(scratch_written, (pair * 2 + (b - 1)) * 32)
                    gather(pair * 2 + b, b, pair + 1)

        @block.sync
        def _(sp):
            def write_scratch(t, b, nth):
                sp.wait_ge(gathered[b], nth * (16 * FIELDS))
                for c in range(2):
                    sp.dma_start(
                        fields_dram[c * FIELDS:(c + 1) * FIELDS, bass.ds(t * (P * DIM), P * DIM)].rearrange(
                            "f (p d) -> p f d", d=DIM),
                        emb[b][:, :].rearrange("p (f d) -> p f d", d=DIM)).then_inc(scratch_written, 16)

            def load_block(n, b, reuse):
                cols = bass.ds(n * COLS, COLS)
                if reuse:
                    sp.wait_ge(prod_made, l1_base(n - 2))
                for q in range(QUADS):
                    sp.dma_start(xrep[b][q * FIELDS:(q + 1) * FIELDS, :],
                                 fields_dram[0:FIELDS, cols]).then_inc(xrep_loaded[b], 16)
                for k in range(ROTS):
                    if reuse:
                        sp.wait_ge(prod_made, l1_base(n - 2) + HBLKS * (k + 1))
                    for q in range(QUADS):
                        r = k * QUADS + q
                        sp.dma_start(rot[b][k][q * FIELDS:(q + 1) * FIELDS, :],
                                     fields_dram[r:r + FIELDS, cols]).then_inc(rot_loaded[b][k], 16)

            def load_pair(pair):
                for b in range(2):
                    load_block(pair * 2 + b, b, True)

            write_scratch(0, 0, 1)
            sp.wait_ge(scratch_written, 32)
            for n in range(2):
                load_block(n, n, False)
            TP = TILE_BLOCKS // 2
            def tile(t, b, nth):
                with sp.Fori(1, TP - 1) as j:
                    load_pair(t * TP + j)
                write_scratch(t + 1, b, nth)
                load_pair(t * TP + (TP - 1))
                sp.wait_ge(scratch_written, (t + 2) * 32)
                load_pair(t * TP + TP)

            with sp.Fori(0, (TILES - 2) // 2) as u:
                tile(u * 2, 1, u + 1)
                tile(u * 2 + 1, 0, u + 2)
            tile(TILES - 2, 1, TILES // 2)
            with sp.Fori((TILES - 1) * TP + 1, TILES * TP) as j:
                load_pair(j)
            sp.wait_ge(y_made, MN)
            sp.dma_start(y.rearrange("b o -> o b"), y_sb[0:1, :]).then_inc(y_stored, 16)
            sp.wait_ge(y_stored, 16)

        @block.scalar
        def _(act):
            act.dma_start(w0_sb[:, :, :], w0_first).then_inc(w0_loaded, 16)
            act.dma_start(w0b_sb[:, :, :], w0_second).then_inc(w0_loaded, 16)
            act.dma_start(w0l_sb[:, :, :], w0_left).then_inc(w0_loaded, 16)
            act.dma_start(b0_sb[:, :], b0).then_inc(bias_loaded, 16)
            act.dma_start(b1_sb[:, :], b1).then_inc(bias_loaded, 16)
            act.dma_start(w1_sb[:, :, :], w1).then_inc(w1_loaded, 16)
            act.wait_ge(zeroed, 1)
            act.dma_start(feat0[0:DENSE, :], dense_t).then_inc(top_loaded, 16)
            act.dma_start(wt1_sb[:, :, :], w_top1).then_inc(top_loaded, 16)
            act.dma_start(bt1_sb[:, :], b_top1).then_inc(top_loaded, 16)
            act.dma_start(wt2_sb[:, :, :], w_top2).then_inc(top_loaded, 16)
            act.dma_start(bt2_sb[:, :], b_top2).then_inc(top_loaded, 16)
            act.dma_start(wt3_sb[:, :], w_top3).then_inc(top_loaded, 16)

            def finish_l0(n, b, first=False):
                act.wait_ge(prod_used, L0_STEPS if first else l0_base(n) + L0_STEPS)
                if not first:
                    act.wait_ge(sum0_made, n)
                act.activation(relu0[HID:P, :], out0[HID:P, :], ACT.Relu,
                               bias=b0_sb[HID:P, :]).then_inc(relu0_made, 1)
                if n_two_back(n, first):
                    act.wait_ge(prod_made, l1_base(n - 2) + L1_STEPS)
                for j in range(HBLKS):
                    for q in range(QUADS):
                        h = slice(j * FIELDS, (j + 1) * FIELDS)
                        act.activation(hrep[b][j][q * FIELDS:(q + 1) * FIELDS, :], out0[h, :], ACT.Relu,
                                       bias=b0_sb[h, :]).then_inc(hrep_made, 1)

            def n_two_back(n, first):
                return not first and not (isinstance(n, int) and n < 2)

            def finish_l1(n, first=False, products_before=None):
                before = l1_base(n) if products_before is None else products_before
                act.wait_ge(prod_used, before + L1_STEPS)
                if not first:
                    act.wait_ge(sum1_made, n)
                act.activation(relu1[:, :], out1[:, :], ACT.Relu, bias=b1_sb[:, :]).then_inc(relu1_made, 1)

            act.wait_ge(bias_loaded, 32)
            finish_l0(0, 0, first=True)
            finish_l0(1, 1)
            finish_l1(0, first=True)
            with act.Fori(0, BLOCKS // 2 - 1) as i:
                for u in range(2):
                    finish_l0(i * 2 + (u + 2), u)
                    finish_l1(i * 2 + (u + 1))
            finish_l1(BLOCKS - 1, products_before=(BLOCKS - 1) * STEPS + L0_STEPS)

            act.wait_ge(top_loaded, 96)
            for j in range(C1 * MN):
                c, half = j // MN, j % MN
                act.wait_ge(h1_done, j + 1)
                act.activation(h1_sb[c][:, half * BANK:(half + 1) * BANK], banks[j], ACT.Relu,
                               bias=bt1_sb[:, c:c + 1]).then_inc(h1_made, 1)
            for j in range(C2 * MN):
                c, half = j // MN, j % MN
                act.wait_ge(h2_done, j + 1)
                act.activation(h2_sb[:, c, half * BANK:(half + 1) * BANK], banks[j], ACT.Relu,
                               bias=bt2_sb[:, c:c + 1]).then_inc(h2_made, 1)
            for half in range(MN):
                act.wait_ge(y_done, half + 1)
                act.activation(y_sb[0:1, half * BANK:(half + 1) * BANK], banks[C2 * MN + half][0:1, :],
                               ACT.Copy).then_inc(y_made, 1)

        @block.vector
        def _(dve):
            dve.wait_ge(w0_loaded, 48)
            nc.vector.tensor_tensor(w0_sb[FIELDS:HID, 0, :], w0_sb[FIELDS:HID, 0, :], w0b_sb[FIELDS:HID, 0, :],
                                    ALU.add).then_inc(w0_folded, 1)
            nc.vector.tensor_tensor(w0_sb[HID:P, 0, :], w0_sb[HID:P, 0, :], w0b_sb[HID:P, 0, :],
                                    ALU.add).then_inc(w0_folded, 1)
            nc.vector.tensor_tensor(w0_sb[:, 1:L0_FULL, :], w0_sb[:, 1:L0_FULL, :], w0b_sb[:, 1:L0_FULL, :],
                                    ALU.add).then_inc(w0_folded, 1)
            nc.vector.tensor_tensor(w0l_sb[:, 0, :], w0l_sb[:, 0, :], w0l_sb[:, 1, :], ALU.add).then_inc(w0_folded, 1)

            def product(slot, s, rows, in0, in1):
                if not (isinstance(s, int) and s < RING):
                    dve.wait_ge(prod_used, s - (RING - 1))
                nc.vector.tensor_tensor(prod[slot][0:rows, :], in0[0:rows, :], in1[0:rows, :],
                                        ALU.mult).then_inc(prod_made, 1)

            def products_l0(s, slot, nth, b):
                dve.wait_ge(xrep_loaded[b], nth * (16 * QUADS))
                for k in range(L0_STEPS):
                    dve.wait_ge(rot_loaded[b][k], nth * (16 * QUADS))
                    product((slot + k) % RING, s + k, P if k < L0_FULL else LEFT, xrep[b], rot[b][k])

            def products_l1(s, slot, n, nth, b, after):
                dve.wait_ge(hrep_made, (n + 1) * (HBLKS * QUADS))
                for k in range(ROTS):
                    if k >= L0_STEPS:
                        dve.wait_ge(rot_loaded[b][k], nth * (16 * QUADS))
                    for j in range(HBLKS):
                        step = k * HBLKS + j
                        product((slot + step) % RING, s + step, P, hrep[b][j], rot[b][k])
                    if k == 1:
                        after()

            def sum_l0(n):
                dve.wait_ge(relu0_made, n + 1)
                nc.vector.tensor_reduce(feat0[HID:P, bass.ds(n * ROWS, ROWS)],
                                        relu0[HID:P, :].rearrange("p (r d) -> p r d", d=DIM),
                                        AX.X, ALU.add).then_inc(sum0_made, 1)

            def sum_l1(n):
                dve.wait_ge(relu1_made, n + 1)
                nc.vector.tensor_reduce(feat1[:, bass.ds(n * ROWS, ROWS)],
                                        relu1[:, :].rearrange("p (r d) -> p r d", d=DIM),
                                        AX.X, ALU.add).then_inc(sum1_made, 1)

            def period(n, slot, b, nth, nth_next, first=False):
                products_l0(l0_base(n + 1), slot, nth_next, 1 - b)
                sum_l0(n)
                products_l1(l1_base(n), slot + L0_STEPS, n, nth, b, (lambda: None) if first else (lambda: sum_l1(n - 1)))

            dve.wait_ge(zeroed, 1)
            products_l0(0, 0, 1, 0)
            period(0, L0_STEPS, 0, 1, 1, first=True)
            with dve.Fori(0, BLOCKS // 2 - 1) as i:
                period(i * 2 + 1, L0_STEPS + STEPS, 1, i + 1, i + 2)
                period(i * 2 + 2, L0_STEPS + 2 * STEPS, 0, i + 2, i + 2)
            last = BLOCKS - 1
            sum_l0(last)
            products_l1(l1_base(last) - L0_STEPS, (l1_base(last) - L0_STEPS) % RING, last, BLOCKS // 2, last % 2,
                        lambda: sum_l1(last - 1))
            sum_l1(last)

        @block.tensor
        def _(pe):
            def step(slot, s, rows, w, out, start, stop):
                pe.wait_ge(prod_made, s + 1)
                for half in range(HALVES):
                    c = slice(half * BANK, (half + 1) * BANK)
                    mm = nc.tensor.matmul(out[:, c], w, prod[slot][0:rows, c], start=start, stop=stop)
                mm.then_inc(prod_used, 1)

            def matmuls_l0(s, slot, n):
                if not (isinstance(n, int) and n == 0):
                    pe.wait_ge(relu0_made, n)
                    pe.wait_ge(hrep_made, n * (HBLKS * QUADS))
                for k in range(L0_FULL):
                    step((slot + k) % RING, s + k, P, w0_sb[:, k, :], out0, k == 0, False)
                step((slot + L0_FULL) % RING, s + L0_FULL, LEFT, w0l_sb[:, 0, :], out0, False, True)

            def matmuls_l1(s, slot, n):
                if not (isinstance(n, int) and n == 0):
                    pe.wait_ge(relu1_made, n)
                for k in range(L1_STEPS):
                    step((slot + k) % RING, s + k, P, w1_sb[:, k, :], out1, k == 0, k == L1_STEPS - 1)

            def period(n, slot):
                matmuls_l0(l0_base(n + 1), slot, n + 1)
                matmuls_l1(l1_base(n), slot + L0_STEPS, n)

            pe.wait_ge(w0_folded, 4)
            matmuls_l0(0, 0, 0)
            pe.wait_ge(w1_loaded, 16)
            period(0, L0_STEPS)
            with pe.Fori(0, BLOCKS // 2 - 1) as i:
                period(i * 2 + 1, L0_STEPS + STEPS)
                period(i * 2 + 2, L0_STEPS + 2 * STEPS)
            last = BLOCKS - 1
            matmuls_l1(l1_base(last) - L0_STEPS, (l1_base(last) - L0_STEPS) % RING, last)

            pe.wait_ge(top_loaded, 96)
            pe.wait_ge(sum0_made, BLOCKS)
            pe.wait_ge(sum1_made, BLOCKS)
            for c in range(C1):
                for half in range(MN):
                    cols = slice(half * BANK, (half + 1) * BANK)
                    for k, feat in enumerate((feat0, feat1)):
                        mm = nc.tensor.matmul(banks[c * MN + half], wt1_sb[:, k, c * P:(c + 1) * P], feat[:, cols],
                                              start=k == 0, stop=k == 1)
                    mm.then_inc(h1_done, 1)
            pe.wait_ge(h1_made, C1 * MN)
            for c in range(C2):
                for half in range(MN):
                    cols = slice(half * BANK, (half + 1) * BANK)
                    for k in range(C1):
                        mm = nc.tensor.matmul(banks[c * MN + half], wt2_sb[:, k, c * P:(c + 1) * P],
                                              h1_sb[k][:, cols], start=k == 0, stop=k == C1 - 1)
                    mm.then_inc(h2_done, 1)
            pe.wait_ge(h2_made, C2 * MN)
            for half in range(MN):
                cols = slice(half * BANK, (half + 1) * BANK)
                for k in range(C2):
                    mm = nc.tensor.matmul(banks[C2 * MN + half][0:1, :], wt3_sb[:, k:k + 1], h2_sb[:, k, cols],
                                          start=k == 0, stop=k == C2 - 1)
                mm.then_inc(y_done, 1)


def lay_out(inputs):
    a = {name: np.asarray(v) for name, v in inputs.items()}
    i = np.arange(FIELDS)
    w0 = a["L0_rec_W0"].reshape(OUT, FIELDS, FIELDS)
    w1 = a["L0_rec_W1"].reshape(OUT, HID, FIELDS)
    first = np.stack([w0[:, i, (i + r) % FIELDS].T for r in range(LEFT + 1)])
    second = np.stack([w0[:, (i + r) % FIELDS, i].T for r in range(LEFT + 1)])
    w1r = np.stack([np.stack([w1[:, j * FIELDS + i, (i + r) % FIELDS].T for j in range(HBLKS)])
                    for r in range(FIELDS)])
    full = lambda w: w[:LEFT].reshape(L0_FULL, P, OUT).transpose(1, 0, 2)
    top1 = a["W_top1"]
    pad = np.zeros((HID - DENSE, H1), top1.dtype)
    tile0 = np.concatenate([top1[HID + OUT:], pad, top1[:HID]])
    return {
        "ids": a["ids"], "dense_t": a["dense_ctx"].T,
        "w0_first": full(first), "w0_second": full(second),
        "w0_left": np.stack([first[LEFT, :LEFT], second[LEFT, :LEFT]], axis=1),
        "w1": w1r.reshape(ROTS, QUADS, HBLKS, FIELDS, OUT).transpose(1, 3, 0, 2, 4).reshape(P, L1_STEPS, OUT),
        "b0": a["L0_rec_b0"].reshape(P, 1), "b1": a["L0_rec_b1"].reshape(P, 1),
        "w_top1": np.stack([tile0, top1[HID:HID + OUT]], axis=1),
        "b_top1": a["b_top1"].reshape(C1, P).T,
        "w_top2": a["W_top2"].reshape(C1, P, H2).transpose(1, 0, 2),
        "b_top2": a["b_top2"].reshape(C2, P).T,
        "w_top3": a["W_top3"].reshape(C2, P).T,
        **{f"tbl_{f}": a[f"tbl_{f}"] for f in range(FIELDS)},
    }


def kernel(**inputs):
    import concourse.bacc as bacc
    from concourse.bass_utils import run_bass_kernel_spmd

    nc = bacc.Bacc("TRN2", target_bir_lowering=False, num_devices=1)
    arrays, aps = {}, {}
    for name, a in lay_out(inputs).items():
        a = np.ascontiguousarray(a)
        arrays[f"in_{name}"] = a
        aps[name] = nc.dram_tensor(f"in_{name}", a.shape, mybir.dt.from_np(a.dtype), kind="ExternalInput").ap()
    y = nc.dram_tensor("out_y", (BATCH, 1), F32, kind="ExternalOutput").ap()
    tables = [aps.pop(f"tbl_{f}") for f in range(FIELDS)]
    cin_mlp(nc, tables=tables, y=y, **aps)
    r = run_bass_kernel_spmd(nc, [arrays], core_ids=[0])
    return r.results[0]["out_y"]
```

```python
import numpy as np
import concourse.bass as bass
from concourse import mybir
from contextlib import ExitStack

F32 = mybir.dt.float32
I32 = mybir.dt.int32
ALU = mybir.AluOpType
ACT = mybir.ActivationFunctionType
AX = mybir.AxisListType

P = 128
BATCH, FIELDS, DIM, DENSE = 1024, 32, 64, 16
OUT = 128
HID = OUT // 2
QUADS = P // FIELDS
ROWS = 16
COLS = ROWS * DIM
BLOCKS = BATCH // ROWS
BANK = 512
HALVES = COLS // BANK
ROTS = FIELDS // QUADS
L0_FULL = ROTS // 2
LOW = ROTS // 2
LEFT = FIELDS // 2
HBLKS = HID // FIELDS
PAIR = 2
HALF = ROTS // PAIR
L0_STEPS = LOW // PAIR
L1_STEPS = HBLKS * HALF
HREP_OPS = P // HID + QUADS
STEPS = L0_STEPS + L1_STEPS
RING = 5
SPLIT = (0, 1, 2, 4, 5, 6)
POOL_SPLIT = (1, 2, 4, 5, 6)
DVE_SPLIT = 0
PARTS = 3
NS, NPS = len(SPLIT), len(POOL_SPLIT)
L1_ORDER = (0, 1, 2, 3, 7, 4, 5, 6)
F32R = mybir.dt.float32r
GROUP = 4
GROUPS = FIELDS // GROUP
AHEAD = 3
TILES = BATCH // P
TILE_BLOCKS = P // ROWS
assert GROUPS == TILE_BLOCKS and HBLKS == HALVES == PAIR
PITCH = BATCH * DIM + 1024
H1, H2 = 512, 256
C1, C2 = H1 // P, H2 // P
MN = BATCH // BANK



def l0_base(n):
    return L0_STEPS + (n - 1) * STEPS


def l1_base(n):
    return n * STEPS + 2 * L0_STEPS


def l1_used(n, k):
    return l1_base(n) + L1_ORDER.index(k) + 1


def is_past(n, m):
    return not isinstance(n, int) or n > m


def is_first(n):
    return not is_past(n, 0)


LAST = BLOCKS - 1
LAST_BASE = l1_base(LAST) - L0_STEPS
L1_SLOT = [l1_base(b) % RING for b in range(2)]
assert 2 * STEPS % RING == 0


def cin_mlp(nc, ids, dense_t, w0_first, w0_second, w0l_first, w0l_second, w1, b0, b1, w_top1, b_top1, w_top2, b_top2, w_top3,
            tables, y):
    ctx = ExitStack()
    with ctx:
        def sb(name, shape, dt=F32):
            return ctx.enter_context(nc.sbuf_tensor(name, shape, dt))

        def pb(name, shape):
            return ctx.enter_context(nc.psum_tensor(name, shape, F32))

        def sem(name):
            return ctx.enter_context(nc.semaphore(name))

        fields_dram = nc.dram_tensor("fields_dram", (2 * FIELDS, PITCH), F32).ap()

        idx_first = sb("idx_first", [P, FIELDS], I32)
        idx = [sb(f"idx{g}", [P, GROUP], I32) for g in range(GROUPS)]
        emb = sb("emb", [P, FIELDS, DIM])
        rot_low = [sb(f"rot_low{b}", [P, LOW, COLS]) for b in range(2)]
        rot_high = sb("rot_high", [P, ROTS - LOW, COLS])
        xrep = sb("xrep", [P, COLS])
        prod = [sb(f"prod{r}", [P, PAIR, COLS]) for r in range(RING)]
        relu = sb("relu", [P, 2, COLS])
        relu0, relu1 = relu[:, 0, :], relu[:, 1, :]
        zh = [sb(f"zh{u}", [P, PAIR, COLS], F32R) for u in range(PARTS)]
        zl = [sb(f"zl{u}", [P, PAIR, COLS], F32R) for u in range(PARTS)]
        left_x = sb("left_x", [P, BANK])
        left_y = sb("left_y", [P, BANK])
        left_z = sb("left_z", [P, BANK])
        left_parts = sb("left_parts", [P, BANK], F32R)
        w0_sb = sb("w0_sb", [P, LOW, OUT])
        w0b_sb = sb("w0b_sb", [P, LOW, OUT])
        w0l_sb = sb("w0l_sb", [P, HALVES, OUT])
        w0lb_sb = sb("w0lb_sb", [P, HALVES, OUT])
        w0l_parts = sb("w0l_parts", [P, HALVES, OUT], F32R)
        w1h = sb("w1h", [P, NS * PAIR, OUT], F32R)
        w1l = sb("w1l", [P, NS * PAIR, OUT], F32R)
        w1_sb = sb("w1_sb", [P, L1_STEPS * PAIR, OUT])
        b0_sb = sb("b0_sb", [P, 1])
        b1_sb = sb("b1_sb", [P, 1])
        wt1_sb = sb("wt1_sb", [P, 2, H1])
        bt1_sb = sb("bt1_sb", [P, C1])
        wt2_sb = sb("wt2_sb", [P, C1, H2])
        bt2_sb = sb("bt2_sb", [P, C2])
        wt3_sb = sb("wt3_sb", [P, C2])
        feat0 = sb("feat0", [P, BATCH])
        feat1 = sb("feat1", [P, BATCH])
        h1_sb = [prod[c // PAIR][:, c % PAIR, :] for c in range(C1)]
        h2_sb = relu
        y_sb = prod[C1 // PAIR][0:1, 0, :]

        out0 = pb("out0", [P, COLS])
        out1 = pb("out1", [P, COLS])
        hrep = pb("hrep", [P, HBLKS, COLS])
        banks = [hrep[:, j // HALVES, (j % HALVES) * BANK:(j % HALVES + 1) * BANK] for j in range(4)] + \
                [out0[:, j * BANK:(j + 1) * BANK] for j in range(2)] + \
                [out1[:, j * BANK:(j + 1) * BANK] for j in range(2)]

        idx_first_loaded = sem("idx_first_loaded")
        idx_loaded = [sem(f"idx_loaded{g}") for g in range(GROUPS)]
        group_started = sem("group_started")
        gathered = [sem(f"gathered{g}") for g in range(GROUPS)]
        scratch_written = [sem(f"scratch_written{g}") for g in range(GROUPS)]
        xrep_loaded = sem("xrep_loaded")
        left_loaded = sem("left_loaded")
        rot_low_loaded = [[sem(f"rot_low_loaded{b}_{t}") for t in range(L0_STEPS)] for b in range(2)]
        rot_high_loaded = [sem(f"rot_high_loaded{t}") for t in range(L0_STEPS, HALF)]
        w0_loaded = sem("w0_loaded")
        w1_loaded = sem("w1_loaded")
        bias_loaded = sem("bias_loaded")
        top_loaded = sem("top_loaded")
        w0_folded = sem("w0_folded")
        w0l_rounded = sem("w0l_rounded")
        w0l_split = sem("w0l_split")
        w1_rounded = sem("w1_rounded")
        w1_split = sem("w1_split")
        zeroed = sem("zeroed")
        prod_made = sem("prod_made")
        prod_used = sem("prod_used")
        split_rounded = sem("split_rounded")
        pool_split_made = sem("pool_split_made")
        dve_split_made = sem("dve_split_made")
        left_made = sem("left_made")
        left_rounded = sem("left_rounded")
        left_split = sem("left_split")
        left_used = sem("left_used")
        relu0_made = sem("relu0_made")
        relu1_made = sem("relu1_made")
        hrep_made = sem("hrep_made")
        sum0_made = sem("sum0_made")
        sum1_made = sem("sum1_made")
        h1_done = sem("h1_done")
        h1_made = sem("h1_made")
        h2_done = sem("h2_done")
        h2_made = sem("h2_made")
        y_done = sem("y_done")
        y_made = sem("y_made")
        y_stored = sem("y_stored")

        block = ctx.enter_context(nc.Block())

        def split_made(n, k):
            if k == DVE_SPLIT:
                return dve_split_made, n + 1
            return pool_split_made, n * NPS + (POOL_SPLIT.index(k) + 1)

        def over_tiles(eng, period, end):
            full = TILES - 2
            with eng.Fori(0, full) as i:
                for v in range(TILE_BLOCKS):
                    period(i * TILE_BLOCKS + v, v, i + (1 + (v + AHEAD) // GROUPS))
            start = full * TILE_BLOCKS
            tail = start + TILE_BLOCKS - 1
            for n in range(start, tail):
                v = n % TILE_BLOCKS
                period(n, v, TILES - 1 if v + AHEAD < GROUPS else None)
            pairs = (end - tail) // 2
            with eng.Fori(0, pairs) as i:
                for u in range(2):
                    period(i * 2 + (tail + u), TILE_BLOCKS - 1 + u, None)
            for n in range(tail + 2 * pairs, end):
                period(n, n % TILE_BLOCKS, None)

        @block.gpsimd
        def _(pool):
            def gather(f, src, c):
                pool.indirect_dma_start(
                    out=emb[:, f, :], out_offset=None, in_=tables[f],
                    in_offset=bass.IndirectOffsetOnAxis(ap=src[:, c:c + 1], axis=0),
                ).then_inc(gathered[f // GROUP], 16)

            def load_idx(g, tile):
                pool.dma_start(idx[g][:, :], ids[bass.ds(tile * P, P), g * GROUP:(g + 1) * GROUP]
                               ).then_inc(idx_loaded[g], 16)

            def gather_group(g, tile):
                pool.wait_ge(idx_loaded[g], tile * 16)
                pool.sem_inc(group_started, 1)
                for c in range(GROUP):
                    gather(g * GROUP + c, idx[g], c)

            def split(n, k, slot):
                u = SPLIT.index(k)
                pool.wait_ge(split_rounded, n * NS + (u + 1))
                pool.tensor_tensor(zl[u % PARTS][:, :, :], prod[(slot + k) % RING][:, :, :],
                                   zh[u % PARTS][:, :, :].bitcast(F32), ALU.subtract).then_inc(pool_split_made, 1)

            def period(n, v, tile):
                slot = L1_SLOT[v % 2]
                for k in POOL_SPLIT:
                    split(n, k, slot)
                if tile is not None:
                    g = (v + AHEAD) % GROUPS
                    gather_group(g, tile)
                    if not (isinstance(tile, int) and g == GROUPS - 1):
                        after, tile_after = (g + 1) % GROUPS, tile + (g + 1) // GROUPS
                        pool.wait_ge(scratch_written[after], tile_after * 32)
                        load_idx(after, tile_after)

            pool.wait_ge(idx_first_loaded, 16)
            for f in range(FIELDS):
                gather(f, idx_first, f)
            for g in range(AHEAD + 1):
                load_idx(g, 1)
            for g in range(AHEAD):
                pool.wait_ge(scratch_written[g], 32)
                gather_group(g, 1)
            pool.wait_ge(scratch_written[AHEAD], 32)
            over_tiles(pool, period, LAST)
            for k in POOL_SPLIT:
                split(LAST, k, LAST_BASE)

        @block.sync
        def _(sp):
            def write_scratch(t, g):
                sp.wait_ge(gathered[g], (t + 1) * (16 * GROUP))
                for c in range(2):
                    row = c * FIELDS + g * GROUP
                    sp.dma_start(
                        fields_dram[row:row + GROUP, bass.ds(t * (P * DIM), P * DIM)].rearrange(
                            "f (p d) -> p f d", d=DIM),
                        emb[:, g * GROUP:(g + 1) * GROUP, :]).then_inc(scratch_written[g], 16)

            def scratch_ready(n):
                for g in range(GROUPS):
                    sp.wait_ge(scratch_written[g], n * (32 // TILE_BLOCKS) + 32)

            def load_rotations(n, t, tile, loaded):
                for q in range(QUADS):
                    row = t * PAIR * QUADS + q
                    rows = fields_dram[row:row + FIELDS, bass.ds(n * COLS, COLS)]
                    both = bass.AP(tensor=rows.tensor, offset=rows.offset,
                                   ap=[[PITCH, FIELDS], [QUADS * PITCH, PAIR], [1, COLS]])
                    sp.dma_start(tile[q * FIELDS:(q + 1) * FIELDS, :, :], both).then_inc(loaded, 16)

            def load_l0(n, b, new_tile=False):
                cols = bass.ds(n * COLS, COLS)
                if not is_first(n):
                    sp.wait_ge(left_made, n)
                if new_tile:
                    scratch_ready(n)
                for tile, row in ((left_x, 0), (left_y, LEFT)):
                    for q in range(QUADS):
                        sp.dma_start(tile[q * FIELDS:(q + 1) * FIELDS, :],
                                     fields_dram[row:row + LEFT, cols].rearrange("i (h c) -> h i c", h=HALVES)
                                     ).then_inc(left_loaded, 16)
                if not is_first(n):
                    sp.wait_ge(prod_made, l0_base(n - 1) + L0_STEPS if is_past(n, 1) else L0_STEPS)
                for q in range(QUADS):
                    sp.dma_start(xrep[q * FIELDS:(q + 1) * FIELDS, :], fields_dram[0:FIELDS, cols]
                                 ).then_inc(xrep_loaded, 16)
                for t in range(L0_STEPS):
                    if is_past(n, 1):
                        sp.wait_ge(prod_made, l1_base(n - 2) + (HALF + t + 1))
                    load_rotations(n, t, rot_low[b][:, t * PAIR:(t + 1) * PAIR, :], rot_low_loaded[b][t])

            def load_high(n):
                for t in range(L0_STEPS, HALF):
                    if not is_first(n):
                        sp.wait_ge(prod_made, l1_base(n - 1) + (HALF + t + 1))
                    at = (t - L0_STEPS) * PAIR
                    load_rotations(n, t, rot_high[:, at:at + PAIR, :], rot_high_loaded[t - L0_STEPS])

            def period(n, v, tile):
                load_l0(n + 2, v % 2, new_tile=v == TILE_BLOCKS - 2)
                load_high(n + 1)
                if tile is not None:
                    write_scratch(tile, (v + AHEAD) % GROUPS)

            sp.dma_start(idx_first[:, :], ids[0:P, :]).then_inc(idx_first_loaded, 16)
            for g in range(GROUPS):
                write_scratch(0, g)
            for n in range(2):
                load_l0(n, n, new_tile=n == 0)
            load_high(0)
            for g in range(AHEAD):
                write_scratch(1, g)
            over_tiles(sp, period, LAST - 1)
            load_high(LAST)
            sp.wait_ge(y_made, MN)
            sp.dma_start(y.rearrange("b o -> o b"), y_sb[0:1, :]).then_inc(y_stored, 16)
            sp.wait_ge(y_stored, 16)

        @block.scalar
        def _(act):
            act.dma_start(w0_sb[:, :, :], w0_first).then_inc(w0_loaded, 16)
            act.dma_start(w0b_sb[:, :, :], w0_second).then_inc(w0_loaded, 16)
            act.dma_start(w0l_sb[:, :, :], w0l_first).then_inc(w0_loaded, 16)
            act.dma_start(w0lb_sb[:, :, :], w0l_second).then_inc(w0_loaded, 16)
            act.dma_start(b0_sb[:, :], b0).then_inc(bias_loaded, 16)
            act.dma_start(b1_sb[:, :], b1).then_inc(bias_loaded, 16)
            act.dma_start(w1_sb[:, :, :], w1).then_inc(w1_loaded, 16)
            act.wait_ge(zeroed, 1)
            act.dma_start(feat0[0:DENSE, :], dense_t).then_inc(top_loaded, 16)
            act.dma_start(wt1_sb[:, :, :], w_top1).then_inc(top_loaded, 16)
            act.dma_start(bt1_sb[:, :], b_top1).then_inc(top_loaded, 16)
            act.dma_start(wt2_sb[:, :, :], w_top2).then_inc(top_loaded, 16)
            act.dma_start(bt2_sb[:, :], b_top2).then_inc(top_loaded, 16)
            act.dma_start(wt3_sb[:, :], w_top3).then_inc(top_loaded, 16)

            def finish_l0(n):
                act.wait_ge(left_used, n + 1)
                if not is_first(n):
                    act.wait_ge(sum0_made, n)
                act.activation(relu0[HID:P, :], out0[HID:P, :], ACT.Relu,
                               bias=b0_sb[HID:P, :]).then_inc(relu0_made, 1)

            def replicate_h(n, j):
                if j == 0:
                    act.wait_ge(left_used, n + 1)
                if not is_first(n):
                    act.wait_ge(prod_made, l1_base(n - 1) + (j + 1) * HALF)
                rows = HID if j == 0 else FIELDS
                for c in range(P // rows):
                    to = slice(c * rows, (c + 1) * rows)
                    h = slice(0, HID) if j == 0 else slice((c + j) % HBLKS * FIELDS, ((c + j) % HBLKS + 1) * FIELDS)
                    act.activation(hrep[to, j, :], out0[h, :], ACT.Relu, bias=b0_sb[h, :]).then_inc(hrep_made, 1)

            def finish_l1(n, base=None):
                base = l1_base(n) if base is None else base
                act.wait_ge(prod_used, base + L1_STEPS)
                if not is_first(n):
                    act.wait_ge(sum1_made, n)
                act.activation(relu1[:, :], out1[:, :], ACT.Relu, bias=b1_sb[:, :]).then_inc(relu1_made, 1)

            def round_left(n):
                act.wait_ge(left_made, n + 1)
                if not is_first(n):
                    act.wait_ge(left_used, n)
                act.activation(left_parts[:, :], left_z[:, :], ACT.Copy).then_inc(left_rounded, 1)

            def round_split(n, k, slot, base=None):
                base = l1_base(n) if base is None else base
                u = SPLIT.index(k)
                act.wait_ge(prod_made, base + (k + 1))
                if u >= PARTS:
                    act.wait_ge(prod_used, base + (L1_ORDER.index(SPLIT[u - PARTS]) + 1))
                elif not is_first(n):
                    before = max(w for w in range(NS) if w % PARTS == u)
                    act.wait_ge(prod_used, l1_used(n - 1, SPLIT[before]))
                act.activation(zh[u % PARTS][:, :, :], prod[(slot + k) % RING][:, :, :],
                               ACT.Copy).then_inc(split_rounded, 1)

            def period(n, b):
                slot = L1_SLOT[b]
                round_left(n + 1)
                for u in range(2):
                    round_split(n, SPLIT[u], slot)
                if not is_first(n):
                    finish_l1(n - 1)
                round_split(n, SPLIT[2], slot)
                finish_l0(n + 1)
                replicate_h(n + 1, 0)
                for u in range(3, NS):
                    round_split(n, SPLIT[u], slot)
                replicate_h(n + 1, 1)

            act.wait_ge(w0_folded, 4)
            act.activation(w0l_parts[:, :, :], w0l_sb[:, :, :], ACT.Copy).then_inc(w0l_rounded, 1)
            act.wait_ge(w1_loaded, 16)
            for u in range(NS):
                act.activation(w1h[:, u * PAIR:(u + 1) * PAIR, :],
                               w1_sb[:, SPLIT[u] * PAIR:(SPLIT[u] + 1) * PAIR, :], ACT.Copy).then_inc(w1_rounded, 1)
            act.wait_ge(bias_loaded, 32)
            round_left(0)
            finish_l0(0)
            replicate_h(0, 0)
            replicate_h(0, 1)
            for n in range(3):
                period(n, n % 2)
            with act.Fori(1, BLOCKS // 2 - 1) as i:
                period(i * 2 + 1, 1)
                period(i * 2 + 2, 0)
            finish_l1(LAST - 1)
            for u in range(NS):
                round_split(LAST, SPLIT[u], LAST_BASE, LAST_BASE)
            finish_l1(LAST, LAST_BASE)

            act.wait_ge(top_loaded, 96)
            for j in range(C1 * MN):
                c, half = j // MN, j % MN
                act.wait_ge(h1_done, j + 1)
                act.activation(h1_sb[c][:, half * BANK:(half + 1) * BANK], banks[j], ACT.Relu,
                               bias=bt1_sb[:, c:c + 1]).then_inc(h1_made, 1)
            for j in range(C2 * MN):
                c, half = j // MN, j % MN
                act.wait_ge(h2_done, j + 1)
                act.activation(h2_sb[:, c, half * BANK:(half + 1) * BANK], banks[j], ACT.Relu,
                               bias=bt2_sb[:, c:c + 1]).then_inc(h2_made, 1)
            for half in range(MN):
                act.wait_ge(y_done, half + 1)
                act.activation(y_sb[0:1, half * BANK:(half + 1) * BANK], banks[C2 * MN + half][0:1, :],
                               ACT.Copy).then_inc(y_made, 1)

        @block.vector
        def _(dve):
            nc.vector.memset(feat0[:, :], 0.0).then_inc(zeroed, 1)
            dve.wait_ge(w0_loaded, 64)
            for rows, k in ((slice(FIELDS, HID), slice(0, 1)), (slice(HID, P), slice(0, 1)), (slice(0, P), slice(1, LOW))):
                nc.vector.tensor_tensor(w0_sb[rows, k, :], w0_sb[rows, k, :], w0b_sb[rows, k, :],
                                        ALU.add).then_inc(w0_folded, 1)
            nc.vector.tensor_tensor(w0l_sb[:, :, :], w0l_sb[:, :, :], w0lb_sb[:, :, :], ALU.add).then_inc(w0_folded, 1)
            dve.wait_ge(w0l_rounded, 1)
            for q in (1, 3):
                rows = slice(q * FIELDS, (q + 1) * FIELDS)
                nc.vector.tensor_tensor(w0l_parts[rows, :, :], w0l_sb[rows, :, :],
                                        w0l_parts[rows, :, :].bitcast(F32), ALU.subtract).then_inc(w0l_split, 1)
            for u in range(NS):
                dve.wait_ge(w1_rounded, u + 1)
                nc.vector.tensor_tensor(w1l[:, u * PAIR:(u + 1) * PAIR, :],
                                        w1_sb[:, SPLIT[u] * PAIR:(SPLIT[u] + 1) * PAIR, :],
                                        w1h[:, u * PAIR:(u + 1) * PAIR, :].bitcast(F32),
                                        ALU.subtract).then_inc(w1_split, 1)

            def twice(ap):
                return ap.unsqueeze(1).broadcast_to([P, PAIR, COLS])

            def product(slot, in0, in1):
                nc.vector.tensor_tensor(prod[slot % RING][:, :, :], in0, in1, ALU.mult).then_inc(prod_made, 1)

            def wait_l1_freed(n, k):
                if k in SPLIT:
                    dve.wait_ge(*split_made(n, k))
                else:
                    dve.wait_ge(prod_used, l1_used(n, k))

            def products_l0(n, b, slot, nth, before=None):
                dve.wait_ge(left_loaded, (n + 1) * (2 * 16 * QUADS))
                if not is_first(n):
                    dve.wait_ge(left_split, n)
                nc.vector.tensor_tensor(left_z[:, :], left_x[:, :], left_y[:, :], ALU.mult).then_inc(left_made, 1)
                dve.wait_ge(xrep_loaded, (n + 1) * (16 * QUADS))
                for t in range(L0_STEPS):
                    dve.wait_ge(rot_low_loaded[b][t], nth * (16 * QUADS))
                    if before is not None:
                        wait_l1_freed(before, L1_STEPS - RING + t)
                    product(slot + t, twice(xrep[:, :]), rot_low[b][:, t * PAIR:(t + 1) * PAIR, :])
                    if t == 0:
                        dve.wait_ge(left_rounded, n + 1)
                        nc.vector.tensor_tensor(left_parts[HID:P, :], left_z[HID:P, :],
                                                left_parts[HID:P, :].bitcast(F32), ALU.subtract).then_inc(left_split, 1)

            def split(n, slot):
                u = SPLIT.index(DVE_SPLIT)
                dve.wait_ge(split_rounded, n * NS + (u + 1))
                nc.vector.tensor_tensor(zl[u % PARTS][:, :, :], prod[(slot + DVE_SPLIT) % RING][:, :, :],
                                        zh[u % PARTS][:, :, :].bitcast(F32), ALU.subtract).then_inc(dve_split_made, 1)

            def products_l1(n, b, slot, base, l0_steps=L0_STEPS):
                for k in range(L1_STEPS):
                    j, t = k // HALF, k % HALF
                    if t == 0:
                        dve.wait_ge(hrep_made, n * HREP_OPS + (HREP_OPS if j else HREP_OPS - QUADS))
                    if j == 0 and t >= L0_STEPS:
                        dve.wait_ge(rot_high_loaded[t - L0_STEPS], (n + 1) * (16 * QUADS))
                    if k >= RING:
                        if k - RING in SPLIT:
                            dve.wait_ge(*split_made(n, k - RING))
                        else:
                            dve.wait_ge(prod_used, base + (L1_ORDER.index(k - RING) + 1))
                    elif k >= RING - l0_steps:
                        dve.wait_ge(prod_used, base + (k - RING + 1))
                    elif is_first(n):
                        if base + (k - RING + 1) > 0:
                            dve.wait_ge(prod_used, base + (k - RING + 1))
                    else:
                        wait_l1_freed(n - 1, L1_STEPS - RING + l0_steps + k)
                    tiles, at = (rot_low[b], t) if t < L0_STEPS else (rot_high, t - L0_STEPS)
                    product(slot + k, twice(hrep[:, j, :]), tiles[:, at * PAIR:(at + 1) * PAIR, :])
                    if k == DVE_SPLIT + 2:
                        split(n, slot)
                    if k == 5 and not is_first(n):
                        sum_l1(n - 1)

            def sum_l0(n):
                dve.wait_ge(relu0_made, n + 1)
                nc.vector.tensor_reduce(feat0[HID:P, bass.ds(n * ROWS, ROWS)],
                                        relu0[HID:P, :].rearrange("p (r d) -> p r d", d=DIM),
                                        AX.X, ALU.add).then_inc(sum0_made, 1)

            def sum_l1(n):
                dve.wait_ge(relu1_made, n + 1)
                nc.vector.tensor_reduce(feat1[:, bass.ds(n * ROWS, ROWS)],
                                        relu1[:, :].rearrange("p (r d) -> p r d", d=DIM),
                                        AX.X, ALU.add).then_inc(sum1_made, 1)

            def period(n, b, nth_next):
                products_l0(n + 1, 1 - b, L1_SLOT[b] - L0_STEPS, nth_next, None if is_first(n) else n - 1)
                sum_l0(n)
                products_l1(n, b, L1_SLOT[b], l1_base(n))

            products_l0(0, 0, 0, 1)
            period(0, 0, 1)
            with dve.Fori(0, BLOCKS // 2 - 1) as i:
                period(i * 2 + 1, 1, i + 2)
                period(i * 2 + 2, 0, i + 2)
            sum_l0(LAST)
            products_l1(LAST, LAST % 2, LAST_BASE, LAST_BASE, 0)
            sum_l1(LAST)

        @block.tensor
        def _(pe):
            def step(slot, s, w, out, start, stop):
                pe.wait_ge(prod_made, s + 1)
                for j in range(PAIR):
                    for half in range(HALVES):
                        c = slice(half * BANK, (half + 1) * BANK)
                        mm = nc.tensor.matmul(out[:, c], w[:, j, :], prod[slot % RING][:, j, c],
                                              start=start and j == 0, stop=stop and j == PAIR - 1)
                mm.then_inc(prod_used, 1)

            def matmuls_l0(n, s, slot):
                if not is_first(n):
                    pe.wait_ge(relu0_made, n)
                    pe.wait_ge(hrep_made, n * HREP_OPS)
                for t in range(L0_STEPS):
                    step(slot + t, s + t, w0_sb[:, t * PAIR:(t + 1) * PAIR, :], out0, t == 0, False)
                pe.wait_ge(left_split, n + 1)
                for half in range(HALVES):
                    mm = nc.tensor.matmul(out0[:, half * BANK:(half + 1) * BANK], w0l_parts[:, half, :],
                                          left_parts[:, :], start=False, stop=True)
                mm.then_inc(left_used, 1)

            def matmuls_l1(n, s, slot):
                if not is_first(n):
                    pe.wait_ge(relu1_made, n)
                for at, k in enumerate(L1_ORDER):
                    start, stop = at == 0, at == L1_STEPS - 1
                    if k not in SPLIT:
                        step(slot + k, s + k, w1_sb[:, k * PAIR:(k + 1) * PAIR, :], out1, start, stop)
                        continue
                    u = SPLIT.index(k)
                    pe.wait_ge(*split_made(n, k))
                    for j in range(PAIR):
                        for part, (w, z) in enumerate(((w1h, zh[u % PARTS]), (w1l, zh[u % PARTS]), (w1h, zl[u % PARTS]))):
                            for half in range(HALVES):
                                c = slice(half * BANK, (half + 1) * BANK)
                                mm = nc.tensor.matmul(out1[:, c], w[:, u * PAIR + j, :], z[:, j, c],
                                                      start=start and j == 0 and part == 0,
                                                      stop=stop and j == PAIR - 1 and part == 2)
                    mm.then_inc(prod_used, 1)

            def period(n, b):
                matmuls_l0(n + 1, l0_base(n + 1), L1_SLOT[b] - L0_STEPS)
                matmuls_l1(n, l1_base(n), L1_SLOT[b])

            pe.wait_ge(w0_folded, 4)
            pe.wait_ge(w0l_split, 2)
            matmuls_l0(0, 0, 0)
            pe.wait_ge(w1_split, NS)
            period(0, 0)
            with pe.Fori(0, BLOCKS // 2 - 1) as i:
                period(i * 2 + 1, 1)
                period(i * 2 + 2, 0)
            matmuls_l1(LAST, LAST_BASE, LAST_BASE)

            pe.wait_ge(top_loaded, 96)
            pe.wait_ge(sum0_made, BLOCKS)
            pe.wait_ge(sum1_made, BLOCKS)
            for c in range(C1):
                for half in range(MN):
                    cols = slice(half * BANK, (half + 1) * BANK)
                    for k, feat in enumerate((feat0, feat1)):
                        mm = nc.tensor.matmul(banks[c * MN + half], wt1_sb[:, k, c * P:(c + 1) * P], feat[:, cols],
                                              start=k == 0, stop=k == 1)
                    mm.then_inc(h1_done, 1)
            pe.wait_ge(h1_made, C1 * MN)
            for c in range(C2):
                for half in range(MN):
                    cols = slice(half * BANK, (half + 1) * BANK)
                    for k in range(C1):
                        mm = nc.tensor.matmul(banks[c * MN + half], wt2_sb[:, k, c * P:(c + 1) * P],
                                              h1_sb[k][:, cols], start=k == 0, stop=k == C1 - 1)
                    mm.then_inc(h2_done, 1)
            pe.wait_ge(h2_made, C2 * MN)
            for half in range(MN):
                cols = slice(half * BANK, (half + 1) * BANK)
                for k in range(C2):
                    mm = nc.tensor.matmul(banks[C2 * MN + half][0:1, :], wt3_sb[:, k:k + 1], h2_sb[:, k, cols],
                                          start=k == 0, stop=k == C2 - 1)
                mm.then_inc(y_done, 1)


def lay_out(inputs):
    a = {name: np.asarray(v) for name, v in inputs.items()}
    i = np.arange(FIELDS)
    w0 = a["L0_rec_W0"].reshape(OUT, FIELDS, FIELDS)
    w1 = a["L0_rec_W1"].reshape(OUT, HID, FIELDS)
    first = np.stack([w0[:, i, (i + r) % FIELDS].T for r in range(LEFT + 1)])
    second = np.stack([w0[:, (i + r) % FIELDS, i].T for r in range(LEFT + 1)])
    w1r = np.stack([np.stack([w1[:, j * FIELDS + i, (i + r) % FIELDS].T for j in range(HBLKS)])
                    for r in range(FIELDS)])
    w1r = w1r.reshape(ROTS, QUADS, HBLKS, FIELDS, OUT)
    w1q = np.stack([np.stack([w1r[:, q, (q + j) % HBLKS] for j in range(HBLKS)])
                    for q in range(QUADS)])
    full = lambda w: w[:LEFT].reshape(LOW, P, OUT).transpose(1, 0, 2)

    def left(w):
        t = np.zeros((QUADS, HALVES, LEFT, HALVES, OUT), w.dtype)
        for half in range(HALVES):
            t[:, half, :, half, :] = w[LEFT, :LEFT]
        return t.reshape(P, HALVES, OUT)

    top1 = a["W_top1"]
    pad = np.zeros((HID - DENSE, H1), top1.dtype)
    tile0 = np.concatenate([top1[HID + OUT:], pad, top1[:HID]])
    return {
        "ids": a["ids"], "dense_t": a["dense_ctx"].T,
        "w0_first": full(first), "w0_second": full(second),
        "w0l_first": left(first), "w0l_second": left(second),
        "w1": w1q.transpose(0, 3, 1, 2, 4).reshape(P, L1_STEPS * PAIR, OUT),
        "b0": a["L0_rec_b0"].reshape(P, 1), "b1": a["L0_rec_b1"].reshape(P, 1),
        "w_top1": np.stack([tile0, top1[HID:HID + OUT]], axis=1),
        "b_top1": a["b_top1"].reshape(C1, P).T,
        "w_top2": a["W_top2"].reshape(C1, P, H2).transpose(1, 0, 2),
        "b_top2": a["b_top2"].reshape(C2, P).T,
        "w_top3": a["W_top3"].reshape(C2, P).T,
        **{f"tbl_{f}": a[f"tbl_{f}"] for f in range(FIELDS)},
    }


def kernel(**inputs):
    import concourse.bacc as bacc
    from concourse.bass_utils import run_bass_kernel_spmd

    nc = bacc.Bacc("TRN2", target_bir_lowering=False, num_devices=1)
    arrays, aps = {}, {}
    for name, a in lay_out(inputs).items():
        a = np.ascontiguousarray(a)
        arrays[f"in_{name}"] = a
        aps[name] = nc.dram_tensor(f"in_{name}", a.shape, mybir.dt.from_np(a.dtype), kind="ExternalInput").ap()
    y = nc.dram_tensor("out_y", (BATCH, 1), F32, kind="ExternalOutput").ap()
    tables = [aps.pop(f"tbl_{f}") for f in range(FIELDS)]
    cin_mlp(nc, tables=tables, y=y, **aps)
    r = run_bass_kernel_spmd(nc, [arrays], core_ids=[0])
    return r.results[0]["out_y"]
```

```python
import numpy as np
import concourse.bass as bass
from concourse import mybir
from contextlib import ExitStack

F32 = mybir.dt.float32
I32 = mybir.dt.int32
ALU = mybir.AluOpType
ACT = mybir.ActivationFunctionType
AX = mybir.AxisListType

P = 128
BATCH, FIELDS, DIM, DENSE = 1024, 32, 64, 16
OUT = 128
HID = OUT // 2
QUADS = P // FIELDS
ROWS = 16
COLS = ROWS * DIM
BLOCKS = BATCH // ROWS
BANK = 512
HALVES = COLS // BANK
ROTS = FIELDS // QUADS
LOW = ROTS // 2
LEFT = FIELDS // 2
HBLKS = HID // FIELDS
PAIR = 2
HALF = ROTS // PAIR
L0_STEPS = LOW // PAIR
L1_STEPS = HBLKS * HALF
HREP_OPS = P // HID + QUADS
WRITTEN = 16 * 2 * FIELDS * ROWS // P
STEPS = L0_STEPS + L1_STEPS
RING = 5
SPLIT = (0, 1, 2, 4, 5, 6)
POOL_SPLIT = (1, 2, 4, 5, 6)
DVE_SPLIT = 0
PARTS = 3
NS, NPS = len(SPLIT), len(POOL_SPLIT)
L1_ORDER = (0, 1, 2, 3, 7, 4, 5, 6)
F32R = mybir.dt.float32r
GATHERS = FIELDS * ROWS // P
GROUP = P // ROWS
AHEAD = 3
assert HBLKS == HALVES == PAIR
PITCH = BATCH * DIM + 1024
H1, H2 = 512, 256
C1, C2 = H1 // P, H2 // P
MN = BATCH // BANK



def l0_base(n):
    return L0_STEPS + (n - 1) * STEPS


def l1_base(n):
    return n * STEPS + 2 * L0_STEPS


def l1_used(n, k):
    return l1_base(n) + L1_ORDER.index(k) + 1


def is_past(n, m):
    return not isinstance(n, int) or n > m


def is_first(n):
    return not is_past(n, 0)


LAST = BLOCKS - 1
LAST_BASE = l1_base(LAST) - L0_STEPS
L1_SLOT = [l1_base(b) % RING for b in range(2)]
assert 2 * STEPS % RING == 0


def cin_mlp(nc, ids, first_row, tables, dense_t, w0_first, w0_second, w0l_first, w0l_second, w1, b0, b1,
            w_top1, b_top1, w_top2, b_top2, w_top3, y):
    ctx = ExitStack()
    with ctx:
        def sb(name, shape, dt=F32):
            return ctx.enter_context(nc.sbuf_tensor(name, shape, dt))

        def pb(name, shape):
            return ctx.enter_context(nc.psum_tensor(name, shape, F32))

        def sem(name):
            return ctx.enter_context(nc.semaphore(name))

        fields_dram = nc.dram_tensor("fields_dram", (2 * FIELDS, PITCH), F32).ap()

        ids_sb = sb("ids_sb", [P, BLOCKS * GATHERS], I32)
        first_row_sb = sb("first_row_sb", [P, GATHERS], I32)
        idx = [sb(f"idx{b}", [P, GATHERS], I32) for b in range(2)]
        emb = [sb(f"emb{b}", [P, GATHERS, DIM]) for b in range(2)]
        rot_low = [sb(f"rot_low{b}", [P, LOW, COLS]) for b in range(2)]
        rot_high = sb("rot_high", [P, ROTS - LOW, COLS])
        xrep = sb("xrep", [P, COLS])
        prod = [sb(f"prod{r}", [P, PAIR, COLS]) for r in range(RING)]
        relu = sb("relu", [P, 2, COLS])
        relu0, relu1 = relu[:, 0, :], relu[:, 1, :]
        zh = [sb(f"zh{u}", [P, PAIR, COLS], F32R) for u in range(PARTS)]
        zl = [sb(f"zl{u}", [P, PAIR, COLS], F32R) for u in range(PARTS)]
        left_x = sb("left_x", [P, BANK])
        left_y = sb("left_y", [P, BANK])
        left_z = sb("left_z", [P, BANK])
        left_parts = sb("left_parts", [P, BANK], F32R)
        w0_sb = sb("w0_sb", [P, LOW, OUT])
        w0b_sb = sb("w0b_sb", [P, LOW, OUT])
        w0l_sb = sb("w0l_sb", [P, HALVES, OUT])
        w0lb_sb = sb("w0lb_sb", [P, HALVES, OUT])
        w0l_parts = sb("w0l_parts", [P, HALVES, OUT], F32R)
        w1h = sb("w1h", [P, NS * PAIR, OUT], F32R)
        w1l = sb("w1l", [P, NS * PAIR, OUT], F32R)
        w1_sb = sb("w1_sb", [P, L1_STEPS * PAIR, OUT])
        b0_sb = sb("b0_sb", [P, 1])
        b1_sb = sb("b1_sb", [P, 1])
        wt1_sb = sb("wt1_sb", [P, 2, H1])
        bt1_sb = sb("bt1_sb", [P, C1])
        wt2_sb = sb("wt2_sb", [P, C1, H2])
        bt2_sb = sb("bt2_sb", [P, C2])
        wt3_sb = sb("wt3_sb", [P, C2])
        sums0 = w0b_sb[:, :, :].rearrange("p k o -> p (k o)")
        feat0 = sb("feat0", [P, BATCH])
        feat1 = sb("feat1", [P, BATCH])
        h1_sb = [prod[c // PAIR][:, c % PAIR, :] for c in range(C1)]
        h2_sb = relu
        y_sb = prod[C1 // PAIR][0:1, 0, :]

        out0 = pb("out0", [P, COLS])
        out1 = pb("out1", [P, COLS])
        hrep = pb("hrep", [P, HBLKS, COLS])
        banks = [hrep[:, j // HALVES, (j % HALVES) * BANK:(j % HALVES + 1) * BANK] for j in range(4)] + \
                [out0[:, j * BANK:(j + 1) * BANK] for j in range(2)] + \
                [out1[:, j * BANK:(j + 1) * BANK] for j in range(2)]

        ids_loaded = sem("ids_loaded")
        idx_made = sem("idx_made")
        gather_started = sem("gather_started")
        gathered = [sem(f"gathered{b}") for b in range(2)]
        scratch_written = [sem(f"scratch_written{b}") for b in range(2)]
        xrep_loaded = sem("xrep_loaded")
        left_loaded = sem("left_loaded")
        rot_low_loaded = [[sem(f"rot_low_loaded{b}_{t}") for t in range(L0_STEPS)] for b in range(2)]
        rot_high_loaded = [sem(f"rot_high_loaded{t}") for t in range(L0_STEPS, HALF)]
        w0_loaded = sem("w0_loaded")
        w1_loaded = sem("w1_loaded")
        bias_loaded = sem("bias_loaded")
        top_loaded = sem("top_loaded")
        w0_folded = sem("w0_folded")
        w0l_rounded = sem("w0l_rounded")
        w0l_split = sem("w0l_split")
        w1_rounded = sem("w1_rounded")
        w1_split = sem("w1_split")
        zeroed = sem("zeroed")
        prod_made = sem("prod_made")
        prod_used = sem("prod_used")
        split_rounded = sem("split_rounded")
        pool_split_made = sem("pool_split_made")
        dve_split_made = sem("dve_split_made")
        left_made = sem("left_made")
        left_rounded = sem("left_rounded")
        left_split = sem("left_split")
        left_used = sem("left_used")
        relu0_made = sem("relu0_made")
        relu1_made = sem("relu1_made")
        hrep_made = sem("hrep_made")
        sum0_made = sem("sum0_made")
        sum1_made = sem("sum1_made")
        feat0_made = sem("feat0_made")
        h1_done = sem("h1_done")
        h1_made = sem("h1_made")
        h2_done = sem("h2_done")
        h2_made = sem("h2_made")
        y_done = sem("y_done")
        y_made = sem("y_made")
        y_stored = sem("y_stored")

        block = ctx.enter_context(nc.Block())

        def split_made(n, k):
            if k == DVE_SPLIT:
                return dve_split_made, n + 1
            return pool_split_made, n * NPS + (POOL_SPLIT.index(k) + 1)

        @block.gpsimd
        def _(pool):
            def gather(n, b, nth):
                if not (isinstance(nth, int) and nth == 1):
                    pool.wait_ge(scratch_written[b], (nth - 1) * WRITTEN)
                pool.tensor_tensor(idx[b][:, :], ids_sb[:, bass.ds(n * GATHERS, GATHERS)], first_row_sb[:, :],
                                   ALU.add).then_inc(idx_made, 1)
                pool.wait_ge(idx_made, n + 1)
                pool.sem_inc(gather_started, 1)
                for g in range(GATHERS):
                    pool.indirect_dma_start(
                        out=emb[b][:, g, :], out_offset=None, in_=tables,
                        in_offset=bass.IndirectOffsetOnAxis(ap=idx[b][:, g:g + 1], axis=0),
                    ).then_inc(gathered[b], 16)

            def split(n, k, slot):
                u = SPLIT.index(k)
                pool.wait_ge(split_rounded, n * NS + (u + 1))
                pool.tensor_tensor(zl[u % PARTS][:, :, :], prod[(slot + k) % RING][:, :, :],
                                   zh[u % PARTS][:, :, :].bitcast(F32), ALU.subtract).then_inc(pool_split_made, 1)

            def period(n, b, nth=None):
                if nth is not None:
                    gather(n + AHEAD, 1 - b, nth)
                for k in POOL_SPLIT:
                    split(n, k, L1_SLOT[b])

            pool.wait_ge(ids_loaded, 32)
            for n in range(AHEAD):
                gather(n, n % 2, n // 2 + 1)
            period(0, 0, 2)
            with pool.Fori(0, BLOCKS // 2 - 2) as i:
                period(i * 2 + 1, 1, i + 3)
                period(i * 2 + 2, 0, i + 3)
            for n in range(LAST - 2, LAST):
                period(n, n % 2)
            for k in POOL_SPLIT:
                split(LAST, k, LAST_BASE)

        @block.sync
        def _(sp):
            def write_scratch(n, b, nth):
                sp.wait_ge(gathered[b], nth * (16 * GATHERS))
                for g in range(GATHERS):
                    for c in range(2):
                        row = c * FIELDS + g * GROUP
                        sp.dma_start(
                            fields_dram[row:row + GROUP, bass.ds(n * COLS, COLS)].rearrange("f (r d) -> f r d", d=DIM),
                            emb[b][:, g, :]).then_inc(scratch_written[b], 16)

            def load_quadrants(n, dst, row, shift, loaded):
                rows = fields_dram[row:row + FIELDS, bass.ds(n * COLS, COLS)]
                src = bass.AP(tensor=rows.tensor, offset=rows.offset,
                              ap=[[shift * PITCH, QUADS], [PITCH, FIELDS], [1, COLS]])
                sp.dma_start(dst, src).then_inc(loaded, 16)

            def load_rotations(n, t, tile, loaded):
                for j in range(PAIR):
                    load_quadrants(n, tile[:, j, :], (t * PAIR + j) * QUADS, 1, loaded)

            def load_l0(n, b, nth):
                cols = bass.ds(n * COLS, COLS)
                sp.wait_ge(scratch_written[b], nth * WRITTEN)
                if not is_first(n):
                    sp.wait_ge(prod_made, l0_base(n - 1) + L0_STEPS if is_past(n, 1) else L0_STEPS)
                load_quadrants(n, xrep[:, :], 0, 0, xrep_loaded)
                for t in range(L0_STEPS):
                    if is_past(n, 1):
                        sp.wait_ge(prod_made, l1_base(n - 2) + (HALF + t + 1))
                    load_rotations(n, t, rot_low[b][:, t * PAIR:(t + 1) * PAIR, :], rot_low_loaded[b][t])
                if not is_first(n):
                    sp.wait_ge(left_made, n)
                for tile, row in ((left_x, 0), (left_y, LEFT)):
                    for q in range(QUADS):
                        sp.dma_start(tile[q * FIELDS:(q + 1) * FIELDS, :],
                                     fields_dram[row:row + LEFT, cols].rearrange("i (h c) -> h i c", h=HALVES)
                                     ).then_inc(left_loaded, 16)

            def load_high(n):
                for t in range(L0_STEPS, HALF):
                    if not is_first(n):
                        sp.wait_ge(prod_made, l1_base(n - 1) + (HALF + t + 1))
                    at = (t - L0_STEPS) * PAIR
                    load_rotations(n, t, rot_high[:, at:at + PAIR, :], rot_high_loaded[t - L0_STEPS])

            def period(n, b, nth, nth_write=None):
                load_l0(n + 2, b, nth)
                load_high(n + 1)
                if nth_write is not None:
                    write_scratch(n + AHEAD, 1 - b, nth_write)

            sp.dma_start(ids_sb[:, :], ids).then_inc(ids_loaded, 16)
            sp.dma_start(first_row_sb[:, :], first_row).then_inc(ids_loaded, 16)
            write_scratch(0, 0, 1)
            load_l0(0, 0, 1)
            write_scratch(1, 1, 1)
            load_l0(1, 1, 1)
            load_high(0)
            write_scratch(2, 0, 2)
            period(0, 0, 2, 2)
            with sp.Fori(0, BLOCKS // 2 - 2) as i:
                period(i * 2 + 1, 1, i + 2, i + 3)
                period(i * 2 + 2, 0, i + 3, i + 3)
            period(LAST - 2, 1, BLOCKS // 2)
            load_high(LAST)
            sp.wait_ge(y_made, MN)
            sp.dma_start(y.rearrange("b o -> o b"), y_sb[0:1, :]).then_inc(y_stored, 16)
            sp.wait_ge(y_stored, 16)

        @block.scalar
        def _(act):
            act.dma_start(w0_sb[:, :, :], w0_first).then_inc(w0_loaded, 16)
            act.dma_start(w0b_sb[:, :, :], w0_second).then_inc(w0_loaded, 16)
            act.dma_start(w0l_sb[:, :, :], w0l_first).then_inc(w0_loaded, 16)
            act.dma_start(w0lb_sb[:, :, :], w0l_second).then_inc(w0_loaded, 16)
            act.dma_start(b0_sb[:, :], b0).then_inc(bias_loaded, 16)
            act.dma_start(b1_sb[:, :], b1).then_inc(bias_loaded, 16)
            act.dma_start(w1_sb[:, :, :], w1).then_inc(w1_loaded, 16)

            def finish_l0(n, b, pair):
                act.wait_ge(left_used, n + 1)
                if b == 0 and not is_first(n):
                    act.wait_ge(sum0_made, pair)
                act.activation(relu0[b * HID:(b + 1) * HID, :], out0[HID:P, :], ACT.Relu,
                               bias=b0_sb[HID:P, :]).then_inc(relu0_made, 1)

            def replicate_h(n, j):
                if j == 0:
                    act.wait_ge(left_used, n + 1)
                if not is_first(n):
                    act.wait_ge(prod_made, l1_base(n - 1) + (j + 1) * HALF)
                rows = HID if j == 0 else FIELDS
                for c in range(P // rows):
                    to = slice(c * rows, (c + 1) * rows)
                    h = slice(0, HID) if j == 0 else slice((c + j) % HBLKS * FIELDS, ((c + j) % HBLKS + 1) * FIELDS)
                    act.activation(hrep[to, j, :], out0[h, :], ACT.Relu, bias=b0_sb[h, :]).then_inc(hrep_made, 1)

            def finish_l1(n, base=None):
                base = l1_base(n) if base is None else base
                act.wait_ge(prod_used, base + L1_STEPS)
                if not is_first(n):
                    act.wait_ge(sum1_made, n)
                act.activation(relu1[:, :], out1[:, :], ACT.Relu, bias=b1_sb[:, :]).then_inc(relu1_made, 1)

            def round_left(n):
                act.wait_ge(left_made, n + 1)
                if not is_first(n):
                    act.wait_ge(left_used, n)
                act.activation(left_parts[:, :], left_z[:, :], ACT.Copy).then_inc(left_rounded, 1)

            def round_split(n, k, slot, base=None):
                base = l1_base(n) if base is None else base
                u = SPLIT.index(k)
                act.wait_ge(prod_made, base + (k + 1))
                if u >= PARTS:
                    act.wait_ge(prod_used, base + (L1_ORDER.index(SPLIT[u - PARTS]) + 1))
                elif not is_first(n):
                    before = max(w for w in range(NS) if w % PARTS == u)
                    act.wait_ge(prod_used, l1_used(n - 1, SPLIT[before]))
                act.activation(zh[u % PARTS][:, :, :], prod[(slot + k) % RING][:, :, :],
                               ACT.Copy).then_inc(split_rounded, 1)

            def period(n, b, pair_next):
                slot = L1_SLOT[b]
                round_left(n + 1)
                for u in range(2):
                    round_split(n, SPLIT[u], slot)
                if not is_first(n):
                    finish_l1(n - 1)
                round_split(n, SPLIT[2], slot)
                finish_l0(n + 1, 1 - b, pair_next)
                replicate_h(n + 1, 0)
                for u in range(3, NS):
                    round_split(n, SPLIT[u], slot)
                replicate_h(n + 1, 1)

            act.wait_ge(w0_folded, 4)
            act.activation(w0l_parts[:, :, :], w0l_sb[:, :, :], ACT.Copy).then_inc(w0l_rounded, 1)
            act.wait_ge(w1_loaded, 16)
            for u in range(NS):
                act.activation(w1h[:, u * PAIR:(u + 1) * PAIR, :],
                               w1_sb[:, SPLIT[u] * PAIR:(SPLIT[u] + 1) * PAIR, :], ACT.Copy).then_inc(w1_rounded, 1)
            act.wait_ge(bias_loaded, 32)
            round_left(0)
            finish_l0(0, 0, 0)
            replicate_h(0, 0)
            replicate_h(0, 1)
            for n in range(3):
                period(n, n % 2, (n + 1) // 2)
            act.wait_ge(zeroed, 1)
            act.dma_start(feat0[0:DENSE, :], dense_t).then_inc(top_loaded, 16)
            act.dma_start(wt1_sb[:, :, :], w_top1).then_inc(top_loaded, 16)
            act.dma_start(bt1_sb[:, :], b_top1).then_inc(top_loaded, 16)
            act.dma_start(wt2_sb[:, :, :], w_top2).then_inc(top_loaded, 16)
            act.dma_start(bt2_sb[:, :], b_top2).then_inc(top_loaded, 16)
            act.dma_start(wt3_sb[:, :], w_top3).then_inc(top_loaded, 16)
            with act.Fori(1, BLOCKS // 2 - 1) as i:
                period(i * 2 + 1, 1, i + 1)
                period(i * 2 + 2, 0, i + 1)
            for u in range(NS):
                if u == 2:
                    finish_l1(LAST - 1)
                round_split(LAST, SPLIT[u], LAST_BASE, LAST_BASE)
            act.wait_ge(sum0_made, BLOCKS // 2)
            to = feat0[HID:P, :].rearrange("p (m b r) -> p b m r", b=2, r=ROWS)
            for b in range(2):
                act.activation(to[:, b], sums0[b * HID:(b + 1) * HID, :].rearrange("p (m r) -> p m r", r=ROWS),
                               ACT.Copy).then_inc(feat0_made, 1)
            finish_l1(LAST, LAST_BASE)

            act.wait_ge(top_loaded, 96)
            for j in range(C1 * MN):
                c, half = j // MN, j % MN
                act.wait_ge(h1_done, j + 1)
                act.activation(h1_sb[c][:, half * BANK:(half + 1) * BANK], banks[j], ACT.Relu,
                               bias=bt1_sb[:, c:c + 1]).then_inc(h1_made, 1)
            for j in range(C2 * MN):
                c, half = j // MN, j % MN
                act.wait_ge(h2_done, j + 1)
                act.activation(h2_sb[:, c, half * BANK:(half + 1) * BANK], banks[j], ACT.Relu,
                               bias=bt2_sb[:, c:c + 1]).then_inc(h2_made, 1)
            for half in range(MN):
                act.wait_ge(y_done, half + 1)
                act.activation(y_sb[0:1, half * BANK:(half + 1) * BANK], banks[C2 * MN + half][0:1, :],
                               ACT.Copy).then_inc(y_made, 1)

        @block.vector
        def _(dve):
            nc.vector.memset(feat0[:, :], 0.0).then_inc(zeroed, 1)
            dve.wait_ge(w0_loaded, 64)
            for rows, k in ((slice(FIELDS, HID), slice(0, 1)), (slice(HID, P), slice(0, 1)), (slice(0, P), slice(1, LOW))):
                nc.vector.tensor_tensor(w0_sb[rows, k, :], w0_sb[rows, k, :], w0b_sb[rows, k, :],
                                        ALU.add).then_inc(w0_folded, 1)
            nc.vector.tensor_tensor(w0l_sb[:, :, :], w0l_sb[:, :, :], w0lb_sb[:, :, :], ALU.add).then_inc(w0_folded, 1)
            dve.wait_ge(w0l_rounded, 1)
            for q in (1, 3):
                rows = slice(q * FIELDS, (q + 1) * FIELDS)
                nc.vector.tensor_tensor(w0l_parts[rows, :, :], w0l_sb[rows, :, :],
                                        w0l_parts[rows, :, :].bitcast(F32), ALU.subtract).then_inc(w0l_split, 1)
            for u in range(NS):
                dve.wait_ge(w1_rounded, u + 1)
                nc.vector.tensor_tensor(w1l[:, u * PAIR:(u + 1) * PAIR, :],
                                        w1_sb[:, SPLIT[u] * PAIR:(SPLIT[u] + 1) * PAIR, :],
                                        w1h[:, u * PAIR:(u + 1) * PAIR, :].bitcast(F32),
                                        ALU.subtract).then_inc(w1_split, 1)

            def twice(ap):
                return ap.unsqueeze(1).broadcast_to([P, PAIR, COLS])

            def product(slot, in0, in1):
                nc.vector.tensor_tensor(prod[slot % RING][:, :, :], in0, in1, ALU.mult).then_inc(prod_made, 1)

            def wait_l1_freed(n, k):
                if k in SPLIT:
                    dve.wait_ge(*split_made(n, k))
                else:
                    dve.wait_ge(prod_used, l1_used(n, k))

            def products_l0(n, b, slot, nth, before=None):
                dve.wait_ge(xrep_loaded, (n + 1) * 16)
                for t in range(L0_STEPS):
                    dve.wait_ge(rot_low_loaded[b][t], nth * (16 * PAIR))
                    if before is not None:
                        wait_l1_freed(before, L1_STEPS - RING + t)
                    product(slot + t, twice(xrep[:, :]), rot_low[b][:, t * PAIR:(t + 1) * PAIR, :])
                    if t == 0:
                        dve.wait_ge(left_loaded, (n + 1) * (2 * 16 * QUADS))
                        if not is_first(n):
                            dve.wait_ge(left_split, n)
                        nc.vector.tensor_tensor(left_z[:, :], left_x[:, :], left_y[:, :], ALU.mult).then_inc(left_made, 1)
                dve.wait_ge(left_rounded, n + 1)
                nc.vector.tensor_tensor(left_parts[HID:P, :], left_z[HID:P, :],
                                        left_parts[HID:P, :].bitcast(F32), ALU.subtract).then_inc(left_split, 1)

            def split(n, slot):
                u = SPLIT.index(DVE_SPLIT)
                dve.wait_ge(split_rounded, n * NS + (u + 1))
                nc.vector.tensor_tensor(zl[u % PARTS][:, :, :], prod[(slot + DVE_SPLIT) % RING][:, :, :],
                                        zh[u % PARTS][:, :, :].bitcast(F32), ALU.subtract).then_inc(dve_split_made, 1)

            def products_l1(n, b, slot, base, l0_steps=L0_STEPS):
                for k in range(L1_STEPS):
                    j, t = k // HALF, k % HALF
                    if t == 0:
                        dve.wait_ge(hrep_made, n * HREP_OPS + (HREP_OPS if j else HREP_OPS - QUADS))
                    if j == 0 and t >= L0_STEPS:
                        dve.wait_ge(rot_high_loaded[t - L0_STEPS], (n + 1) * (16 * PAIR))
                    if k >= RING:
                        if k - RING in SPLIT:
                            dve.wait_ge(*split_made(n, k - RING))
                        else:
                            dve.wait_ge(prod_used, base + (L1_ORDER.index(k - RING) + 1))
                    elif k >= RING - l0_steps:
                        dve.wait_ge(prod_used, base + (k - RING + 1))
                    elif is_first(n):
                        if base + (k - RING + 1) > 0:
                            dve.wait_ge(prod_used, base + (k - RING + 1))
                    else:
                        wait_l1_freed(n - 1, L1_STEPS - RING + l0_steps + k)
                    tiles, at = (rot_low[b], t) if t < L0_STEPS else (rot_high, t - L0_STEPS)
                    product(slot + k, twice(hrep[:, j, :]), tiles[:, at * PAIR:(at + 1) * PAIR, :])
                    if k == DVE_SPLIT + 2:
                        split(n, slot)
                    if k == 5 and not is_first(n):
                        sum_l1(n - 1)

            def sum_l0(pair):
                dve.wait_ge(relu0_made, (pair + 1) * 2)
                nc.vector.tensor_reduce(sums0[:, bass.ds(pair * ROWS, ROWS)],
                                        relu0[:, :].rearrange("p (r d) -> p r d", d=DIM),
                                        AX.X, ALU.add).then_inc(sum0_made, 1)

            def sum_l1(n):
                dve.wait_ge(relu1_made, n + 1)
                nc.vector.tensor_reduce(feat1[:, bass.ds(n * ROWS, ROWS)],
                                        relu1[:, :].rearrange("p (r d) -> p r d", d=DIM),
                                        AX.X, ALU.add).then_inc(sum1_made, 1)

            def period(n, b, nth_next, pair=None):
                products_l0(n + 1, 1 - b, L1_SLOT[b] - L0_STEPS, nth_next, None if is_first(n) else n - 1)
                if pair is not None:
                    sum_l0(pair)
                products_l1(n, b, L1_SLOT[b], l1_base(n))

            products_l0(0, 0, 0, 1)
            period(0, 0, 1)
            with dve.Fori(0, BLOCKS // 2 - 1) as i:
                period(i * 2 + 1, 1, i + 2, i)
                period(i * 2 + 2, 0, i + 2)
            sum_l0(LAST // 2)
            products_l1(LAST, LAST % 2, LAST_BASE, LAST_BASE, 0)
            sum_l1(LAST)

        @block.tensor
        def _(pe):
            def step(slot, s, w, out, start, stop):
                pe.wait_ge(prod_made, s + 1)
                for j in range(PAIR):
                    for half in range(HALVES):
                        c = slice(half * BANK, (half + 1) * BANK)
                        mm = nc.tensor.matmul(out[:, c], w[:, j, :], prod[slot % RING][:, j, c],
                                              start=start and j == 0, stop=stop and j == PAIR - 1)
                mm.then_inc(prod_used, 1)

            def matmuls_l0(n, s, slot):
                if not is_first(n):
                    pe.wait_ge(relu0_made, n)
                    pe.wait_ge(hrep_made, n * HREP_OPS)
                for t in range(L0_STEPS):
                    step(slot + t, s + t, w0_sb[:, t * PAIR:(t + 1) * PAIR, :], out0, t == 0, False)
                pe.wait_ge(left_split, n + 1)
                for half in range(HALVES):
                    mm = nc.tensor.matmul(out0[:, half * BANK:(half + 1) * BANK], w0l_parts[:, half, :],
                                          left_parts[:, :], start=False, stop=True)
                mm.then_inc(left_used, 1)

            def matmuls_l1(n, s, slot):
                if not is_first(n):
                    pe.wait_ge(relu1_made, n)
                for at, k in enumerate(L1_ORDER):
                    start, stop = at == 0, at == L1_STEPS - 1
                    if k not in SPLIT:
                        step(slot + k, s + k, w1_sb[:, k * PAIR:(k + 1) * PAIR, :], out1, start, stop)
                        continue
                    u = SPLIT.index(k)
                    pe.wait_ge(*split_made(n, k))
                    for j in range(PAIR):
                        for part, (w, z) in enumerate(((w1h, zh[u % PARTS]), (w1l, zh[u % PARTS]), (w1h, zl[u % PARTS]))):
                            for half in range(HALVES):
                                c = slice(half * BANK, (half + 1) * BANK)
                                mm = nc.tensor.matmul(out1[:, c], w[:, u * PAIR + j, :], z[:, j, c],
                                                      start=start and j == 0 and part == 0,
                                                      stop=stop and j == PAIR - 1 and part == 2)
                    mm.then_inc(prod_used, 1)

            def period(n, b):
                matmuls_l0(n + 1, l0_base(n + 1), L1_SLOT[b] - L0_STEPS)
                matmuls_l1(n, l1_base(n), L1_SLOT[b])

            pe.wait_ge(w0_folded, 4)
            pe.wait_ge(w0l_split, 2)
            matmuls_l0(0, 0, 0)
            pe.wait_ge(w1_split, NS)
            period(0, 0)
            with pe.Fori(0, BLOCKS // 2 - 1) as i:
                period(i * 2 + 1, 1)
                period(i * 2 + 2, 0)
            matmuls_l1(LAST, LAST_BASE, LAST_BASE)

            pe.wait_ge(top_loaded, 96)
            pe.wait_ge(feat0_made, 2)
            pe.wait_ge(sum1_made, BLOCKS)
            for c in range(C1):
                for half in range(MN):
                    cols = slice(half * BANK, (half + 1) * BANK)
                    for k, feat in enumerate((feat0, feat1)):
                        mm = nc.tensor.matmul(banks[c * MN + half], wt1_sb[:, k, c * P:(c + 1) * P], feat[:, cols],
                                              start=k == 0, stop=k == 1)
                    mm.then_inc(h1_done, 1)
            pe.wait_ge(h1_made, C1 * MN)
            for c in range(C2):
                for half in range(MN):
                    cols = slice(half * BANK, (half + 1) * BANK)
                    for k in range(C1):
                        mm = nc.tensor.matmul(banks[c * MN + half], wt2_sb[:, k, c * P:(c + 1) * P],
                                              h1_sb[k][:, cols], start=k == 0, stop=k == C1 - 1)
                    mm.then_inc(h2_done, 1)
            pe.wait_ge(h2_made, C2 * MN)
            for half in range(MN):
                cols = slice(half * BANK, (half + 1) * BANK)
                for k in range(C2):
                    mm = nc.tensor.matmul(banks[C2 * MN + half][0:1, :], wt3_sb[:, k:k + 1], h2_sb[:, k, cols],
                                          start=k == 0, stop=k == C2 - 1)
                mm.then_inc(y_done, 1)


def lay_out(inputs):
    a = {name: np.asarray(v) for name, v in inputs.items()}
    i = np.arange(FIELDS)
    w0 = a["L0_rec_W0"].reshape(OUT, FIELDS, FIELDS)
    w1 = a["L0_rec_W1"].reshape(OUT, HID, FIELDS)
    first = np.stack([w0[:, i, (i + r) % FIELDS].T for r in range(LEFT + 1)])
    second = np.stack([w0[:, (i + r) % FIELDS, i].T for r in range(LEFT + 1)])
    w1r = np.stack([np.stack([w1[:, j * FIELDS + i, (i + r) % FIELDS].T for j in range(HBLKS)])
                    for r in range(FIELDS)])
    w1r = w1r.reshape(ROTS, QUADS, HBLKS, FIELDS, OUT)
    w1q = np.stack([np.stack([w1r[:, q, (q + j) % HBLKS] for j in range(HBLKS)])
                    for q in range(QUADS)])
    full = lambda w: w[:LEFT].reshape(LOW, P, OUT).transpose(1, 0, 2)

    def left(w):
        t = np.zeros((QUADS, HALVES, LEFT, HALVES, OUT), w.dtype)
        for half in range(HALVES):
            t[:, half, :, half, :] = w[LEFT, :LEFT]
        return t.reshape(P, HALVES, OUT)

    stacked = [a[f"tbl_{f}"] for f in range(FIELDS)]
    first_row = np.array([sum(t.shape[0] for t in stacked[:f]) for f in range(FIELDS)], np.int32)
    top1 = a["W_top1"]
    pad = np.zeros((HID - DENSE, H1), top1.dtype)
    tile0 = np.concatenate([top1[HID + OUT:], pad, top1[:HID]])
    return {
        "ids": a["ids"].reshape(BLOCKS, ROWS, GATHERS, GROUP).transpose(3, 1, 0, 2).reshape(P, BLOCKS * GATHERS),
        "first_row": np.repeat(first_row.reshape(GATHERS, GROUP).T, ROWS, axis=0),
        "dense_t": a["dense_ctx"].T,
        "w0_first": full(first), "w0_second": full(second),
        "w0l_first": left(first), "w0l_second": left(second),
        "w1": w1q.transpose(0, 3, 1, 2, 4).reshape(P, L1_STEPS * PAIR, OUT),
        "b0": a["L0_rec_b0"].reshape(P, 1), "b1": a["L0_rec_b1"].reshape(P, 1),
        "w_top1": np.stack([tile0, top1[HID:HID + OUT]], axis=1),
        "b_top1": a["b_top1"].reshape(C1, P).T,
        "w_top2": a["W_top2"].reshape(C1, P, H2).transpose(1, 0, 2),
        "b_top2": a["b_top2"].reshape(C2, P).T,
        "w_top3": a["W_top3"].reshape(C2, P).T,
        "tables": np.concatenate(stacked),
    }


def kernel(**inputs):
    import concourse.bacc as bacc
    from concourse.bass_utils import run_bass_kernel_spmd

    nc = bacc.Bacc("TRN2", target_bir_lowering=False, num_devices=1)
    arrays, aps = {}, {}
    for name, a in lay_out(inputs).items():
        a = np.ascontiguousarray(a)
        arrays[f"in_{name}"] = a
        aps[name] = nc.dram_tensor(f"in_{name}", a.shape, mybir.dt.from_np(a.dtype), kind="ExternalInput").ap()
    y = nc.dram_tensor("out_y", (BATCH, 1), F32, kind="ExternalOutput").ap()
    cin_mlp(nc, y=y, **aps)
    r = run_bass_kernel_spmd(nc, [arrays], core_ids=[0])
    return r.results[0]["out_y"]
```
